# Optimizing a Trainium2 kernel written in Bass

```python
import numpy as np
import jax
import jax.numpy as jnp

def _softmax(x, axis=-1):
    return jax.nn.softmax(x, axis=axis)

def _gelu(x):
    return jax.nn.gelu(x, approximate=True)

def _silu(x):
    return jax.nn.silu(x)

def _sigmoid(x):
    return jax.nn.sigmoid(x)

def _layernorm(x, axis=-1, eps=1e-05):
    m = jnp.mean(x, axis=axis, keepdims=True)
    v = jnp.var(x, axis=axis, keepdims=True)
    return (x - m) / jnp.sqrt(v + eps)

def _scatter_add(tgt, idx, src, axis=0):
    return tgt.at[idx].add(src)

def _segment_sum(src, seg, n):
    return jax.ops.segment_sum(src, seg, n)
kernel_name = 'mk_adaln_d1_jaxref_r8_1924a9'

def setup_inputs(seed: int=0):
    np.random.seed(seed)
    _w = jnp.asarray

    def _L0_attn_setup():
        import math
        import jax, jax.numpy as jnp
        import numpy as np
        EMBED_DIM = 256
        NUM_HEADS = 16
        HEAD_DIM = EMBED_DIM // NUM_HEADS
        CHUNK = 128
        RMS_EPS = 1e-05

        def _build_slopes(n):

            def pow2(n):
                start = 2.0 ** (-2.0 ** (-(math.log2(n) - 3)))
                return [start * start ** i for i in range(n)]
            if math.log2(n).is_integer():
                s = pow2(n)
            else:
                closest = 2 ** math.floor(math.log2(n))
                s = pow2(closest) + pow2(2 * closest)[0::2][:n - closest]
            return jnp.asarray(s, dtype=jnp.float32)

        def _rotary(x_BTHD, offset=0):
            T, D = (x_BTHD.shape[1], x_BTHD.shape[-1])
            freq = (1.0 / 1024.0) ** jnp.linspace(0.0, 1.0, D // 4, dtype=jnp.float32)
            freq = jnp.concatenate([freq, jnp.zeros(D // 4, dtype=jnp.float32)])
            t = jnp.arange(offset, offset + T, dtype=jnp.float32)
            theta = t[:, None] * freq[None, :]
            cos = jnp.cos(theta)[None, :, None, :]
            sin = jnp.sin(theta)[None, :, None, :]
            x1, x2 = jnp.split(x_BTHD.astype(jnp.float32), 2, axis=-1)
            y1 = x1 * cos + x2 * sin
            y2 = -x1 * sin + x2 * cos
            return jnp.concatenate([y1, y2], axis=-1).astype(x_BTHD.dtype)

        def _lightning_attn(q, k, v, slopes):
            B, H, T, D = q.shape
            C = CHUNK
            NC = T // C
            r = jnp.exp(-slopes)
            i = jnp.arange(C, dtype=jnp.float32)
            q_decay = r[:, None] ** (i[None, :] + 1.0)
            k_decay = r[:, None] ** (C - 1.0 - i[None, :])
            diff = i[:, None] - i[None, :]
            mask = diff >= 0
            dmask = jnp.where(mask[None], r[:, None, None] ** jnp.where(mask, diff, 0.0)[None], 0.0)
            r_C = r ** float(C)

            def reshape_chunks(x):
                return x.reshape(B, H, NC, C, D).transpose(2, 0, 1, 3, 4)
            qc, kc, vc = (reshape_chunks(q), reshape_chunks(k), reshape_chunks(v))

            def step(kv, qkv):
                qi, ki, vi = qkv
                inter = jnp.einsum('bhcd,bhde->bhce', qi * q_decay[None, :, :, None], kv)
                scores = jnp.einsum('bhcd,bhsd->bhcs', qi, ki) * dmask[None]
                intra = jnp.einsum('bhcs,bhse->bhce', scores, vi)
                kv_new = r_C[None, :, None, None] * kv + jnp.einsum('bhcd,bhce->bhde', ki * k_decay[None, :, :, None], vi)
                return (kv_new, inter + intra)
            kv0 = jnp.zeros((B, H, D, D), dtype=q.dtype)
            _, out = jax.lax.scan(step, kv0, (qc, kc, vc))
            return out.transpose(1, 2, 0, 3, 4).reshape(B, H, T, D)

        def _rms_norm(x, w):
            var = jnp.mean(jnp.square(x), axis=-1, keepdims=True)
            return x * jax.lax.rsqrt(var + RMS_EPS) * w
        key = jax.random.key(seed)
        ks = jax.random.split(key, 6)
        sc = 1.0 / math.sqrt(EMBED_DIM)
        return {'x': jax.random.normal(ks[0], (4, 512, EMBED_DIM), dtype=jnp.float32), 'Wq': jax.random.normal(ks[1], (EMBED_DIM, EMBED_DIM), dtype=jnp.float32) * sc, 'Wk': jax.random.normal(ks[2], (EMBED_DIM, EMBED_DIM), dtype=jnp.float32) * sc, 'Wv': jax.random.normal(ks[3], (EMBED_DIM, EMBED_DIM), dtype=jnp.float32) * sc, 'Wo': jax.random.normal(ks[4], (EMBED_DIM, EMBED_DIM), dtype=jnp.float32) * sc, 'rms_w': jnp.ones((EMBED_DIM,), dtype=jnp.float32)}
    _L0_attn_in = _L0_attn_setup()

    def _L0_ffn_setup():
        import jax, jax.numpy as jnp
        import numpy as np
        NUM_EXPERTS = 8
        RANK = 16
        TOP_K = 2
        SCALING = 32.0 / RANK
        IN_F = 256
        OUT_F = 256
        key = jax.random.key(seed)
        k1, k2, k3, k4, k5 = jax.random.split(key, 5)
        B, T = (4, 256)
        x = jax.random.normal(k1, (B, T, IN_F), dtype=jnp.float32)
        bound_w = 1.0 / np.sqrt(IN_F)
        weight = jax.random.uniform(k2, (OUT_F, IN_F), jnp.float32, -bound_w, bound_w)
        lora_A = jax.random.uniform(k3, (NUM_EXPERTS, RANK, IN_F), jnp.float32, -bound_w, bound_w)
        lora_B = 0.02 * jax.random.normal(k4, (NUM_EXPERTS, OUT_F, RANK), dtype=jnp.float32)
        router_w = jax.random.uniform(k5, (NUM_EXPERTS, IN_F), jnp.float32, -bound_w, bound_w)
        return {'x': x, 'weight': weight, 'lora_A': lora_A, 'lora_B': lora_B, 'router_w': router_w}
    _L0_ffn_in = _L0_ffn_setup()
    _L0_c = _w((lambda *s: np.random.randn(*s).astype(np.float32) * 0.05)(16, 256))
    _L0_wmod = _w((lambda *s: np.random.randn(*s).astype(np.float32) * 0.05)(256, 6 * 256) * 256 ** (-0.5))
    _d = {'L0_attn_x': _L0_attn_in['x'], 'L0_attn_Wq': _L0_attn_in['Wq'], 'L0_attn_Wk': _L0_attn_in['Wk'], 'L0_attn_Wv': _L0_attn_in['Wv'], 'L0_attn_Wo': _L0_attn_in['Wo'], 'L0_attn_rms_w': _L0_attn_in['rms_w'], 'L0_ffn_weight': _L0_ffn_in['weight'], 'L0_ffn_lora_A': _L0_ffn_in['lora_A'], 'L0_ffn_lora_B': _L0_ffn_in['lora_B'], 'L0_ffn_router_w': _L0_ffn_in['router_w'], 'L0_c': _L0_c, 'L0_wmod': _L0_wmod}
    _x0 = _d['L0_attn_x']
    _d['L0_attn_x'] = jax.random.normal(jax.random.fold_in(jax.random.key(seed), 1), (16, 256, 256), dtype=_x0.dtype)
    del _x0
    return _d

def reference(L0_attn_x, L0_attn_Wq, L0_attn_Wk, L0_attn_Wv, L0_attn_Wo, L0_attn_rms_w, L0_ffn_weight, L0_ffn_lora_A, L0_ffn_lora_B, L0_ffn_router_w, L0_c, L0_wmod):

    def _L0_attn_ref(x, Wq, Wk, Wv, Wo, rms_w):
        import math
        import jax, jax.numpy as jnp
        import numpy as np
        EMBED_DIM = 256
        NUM_HEADS = 16
        HEAD_DIM = EMBED_DIM // NUM_HEADS
        CHUNK = 128
        RMS_EPS = 1e-05

        def _build_slopes(n):

            def pow2(n):
                start = 2.0 ** (-2.0 ** (-(math.log2(n) - 3)))
                return [start * start ** i for i in range(n)]
            if math.log2(n).is_integer():
                s = pow2(n)
            else:
                closest = 2 ** math.floor(math.log2(n))
                s = pow2(closest) + pow2(2 * closest)[0::2][:n - closest]
            return jnp.asarray(s, dtype=jnp.float32)

        def _rotary(x_BTHD, offset=0):
            T, D = (x_BTHD.shape[1], x_BTHD.shape[-1])
            freq = (1.0 / 1024.0) ** jnp.linspace(0.0, 1.0, D // 4, dtype=jnp.float32)
            freq = jnp.concatenate([freq, jnp.zeros(D // 4, dtype=jnp.float32)])
            t = jnp.arange(offset, offset + T, dtype=jnp.float32)
            theta = t[:, None] * freq[None, :]
            cos = jnp.cos(theta)[None, :, None, :]
            sin = jnp.sin(theta)[None, :, None, :]
            x1, x2 = jnp.split(x_BTHD.astype(jnp.float32), 2, axis=-1)
            y1 = x1 * cos + x2 * sin
            y2 = -x1 * sin + x2 * cos
            return jnp.concatenate([y1, y2], axis=-1).astype(x_BTHD.dtype)

        def _lightning_attn(q, k, v, slopes):
            B, H, T, D = q.shape
            C = CHUNK
            NC = T // C
            r = jnp.exp(-slopes)
            i = jnp.arange(C, dtype=jnp.float32)
            q_decay = r[:, None] ** (i[None, :] + 1.0)
            k_decay = r[:, None] ** (C - 1.0 - i[None, :])
            diff = i[:, None] - i[None, :]
            mask = diff >= 0
            dmask = jnp.where(mask[None], r[:, None, None] ** jnp.where(mask, diff, 0.0)[None], 0.0)
            r_C = r ** float(C)

            def reshape_chunks(x):
                return x.reshape(B, H, NC, C, D).transpose(2, 0, 1, 3, 4)
            qc, kc, vc = (reshape_chunks(q), reshape_chunks(k), reshape_chunks(v))

            def step(kv, qkv):
                qi, ki, vi = qkv
                inter = jnp.einsum('bhcd,bhde->bhce', qi * q_decay[None, :, :, None], kv)
                scores = jnp.einsum('bhcd,bhsd->bhcs', qi, ki) * dmask[None]
                intra = jnp.einsum('bhcs,bhse->bhce', scores, vi)
                kv_new = r_C[None, :, None, None] * kv + jnp.einsum('bhcd,bhce->bhde', ki * k_decay[None, :, :, None], vi)
                return (kv_new, inter + intra)
            kv0 = jnp.zeros((B, H, D, D), dtype=q.dtype)
            _, out = jax.lax.scan(step, kv0, (qc, kc, vc))
            return out.transpose(1, 2, 0, 3, 4).reshape(B, H, T, D)

        def _rms_norm(x, w):
            var = jnp.mean(jnp.square(x), axis=-1, keepdims=True)
            return x * jax.lax.rsqrt(var + RMS_EPS) * w
        B, T, E = x.shape
        H, D = (NUM_HEADS, HEAD_DIM)
        q = (x @ Wq).reshape(B, T, H, D)
        k = (x @ Wk).reshape(B, T, H, D)
        v = (x @ Wv).reshape(B, T, H, D)
        q = _rotary(q)
        k = _rotary(k)
        q, k, v = (t.transpose(0, 2, 1, 3) for t in (q, k, v))
        slopes = _build_slopes(H)
        attn = _lightning_attn(q, k, v, slopes)
        attn = attn.transpose(0, 2, 1, 3).reshape(B, T, E)
        attn = _rms_norm(attn, rms_w)
        return attn @ Wo

    def _L0_ffn_ref(x, weight, lora_A, lora_B, router_w):
        import jax, jax.numpy as jnp
        import numpy as np
        NUM_EXPERTS = 8
        RANK = 16
        TOP_K = 2
        SCALING = 32.0 / RANK
        IN_F = 256
        OUT_F = 256
        B, T, D = x.shape
        N = B * T
        base = jnp.einsum('btd,od->bto', x, weight)
        logits = jnp.einsum('btd,ed->bte', x, router_w)
        probs = jax.nn.softmax(logits, axis=-1)
        topk_vals, topk_idx = jax.lax.top_k(probs, TOP_K)
        topk_vals = topk_vals / topk_vals.sum(axis=-1, keepdims=True)
        w_dense = jnp.zeros((N, NUM_EXPERTS), dtype=x.dtype).at[jnp.arange(N)[:, None], topk_idx.reshape(N, TOP_K)].set(topk_vals.reshape(N, TOP_K))
        x_flat = x.reshape(N, D)
        Ax = jnp.einsum('nd,erd->ner', x_flat, lora_A)
        expert_out = jnp.einsum('ner,ne,eor->no', Ax, w_dense, lora_B) * SCALING
        return base + expert_out.reshape(B, T, OUT_F)
    x = L0_attn_x
    mod = (_silu(L0_c) @ L0_wmod).reshape(L0_c.shape[0], 6, 1, -1)
    sa, ca, ga, sb, cb, gb = (mod[:, 0], mod[:, 1], mod[:, 2], mod[:, 3], mod[:, 4], mod[:, 5])
    ga = (2 * (ga >= 0) - 1) * jnp.maximum(jnp.abs(ga), 0.25)
    gb = (2 * (gb >= 0) - 1) * jnp.maximum(jnp.abs(gb), 0.25)
    h = _layernorm(x, axis=-1) * (1 + ca) + sa
    x = x + ga * _L0_attn_ref(h, L0_attn_Wq, L0_attn_Wk, L0_attn_Wv, L0_attn_Wo, L0_attn_rms_w)
    h = _layernorm(x, axis=-1) * (1 + cb) + sb
    x = x + gb * _L0_ffn_ref(h, L0_ffn_weight, L0_ffn_lora_A, L0_ffn_lora_B, L0_ffn_router_w)
    return x

_drawn_inputs = setup_inputs


def setup_inputs(seed=0):
    import zlib

    import numpy as np

    out = dict(_drawn_inputs(seed))
    spreads = {'L0_attn_rms_w': (1.0, 0.2)}
    factors = {'L0_ffn_lora_A': 3.567, 'L0_ffn_lora_B': 3.557, 'L0_ffn_router_w': 4.092}
    for name, (base, spread) in spreads.items():
        noise = np.random.default_rng([zlib.crc32(name.encode()), seed]).standard_normal(out[name].shape)
        drawn = base * np.exp(spread * noise) if base else spread * noise
        out[name] = jnp.asarray(drawn.astype(out[name].dtype))
    for name, factor in factors.items():
        out[name] = (out[name] * factor).astype(out[name].dtype)
    return out
```

```python
from contextlib import ExitStack

import concourse.bass as bass
from concourse import mybir

F32 = mybir.dt.float32
F32R = mybir.dt.float32r
ALU = mybir.AluOpType
ACT = mybir.ActivationFunctionType
AX_X = mybir.AxisListType.X

P = 128
NB = 16
NT = 2
E = 256
NH = E // P
H = 16
D = E // H
G = 4
HG = H // G
NE = 8
R = 16
NA = NE * R
EPS = 1e-5
SCALING = 2.0
SA, CA, SB, CB = range(4)


class Batch:

    def __init__(self, first, trip=None):
        self.first, self.trip = first, trip

    def __add__(self, k):
        return Batch(self.first + k, self.trip)

    @property
    def on(self):
        return 0 <= self.first < NB

    @property
    def parity(self):
        return self.first % 2

    def count(self, per=1, extra=1):
        at = per * self.first + extra
        return at if self.trip is None else self.trip * (2 * per) + at

    def at(self):
        return bass.ds(self.count(1, 0), 1)


LOOP_FIRST, LOOP_TRIPS = 4, 5


def pipeline(eng, iteration, first, last):
    for i in range(first, LOOP_FIRST):
        iteration(Batch(i))
    with eng.Fori(0, LOOP_TRIPS) as trip:
        for u in range(2):
            iteration(Batch(LOOP_FIRST + u, trip))
    for i in range(LOOP_FIRST + 2 * LOOP_TRIPS, last + 1):
        iteration(Batch(i))


def hold(eng, semaphore, value, held):
    eng.wait_ge(semaphore, value)
    eng.sem_inc(held, 1)


RING = [("inter", -1), ("t1", 1), ("f2", -2), ("t3", -1), ("qk0", 1), ("wo", -1), ("qk1", 1), ("v", 1),
        ("tq0", 1), ("tk0", 1), ("t4", -1), ("tq1", 1), ("tk1", 1), ("kv", 1), ("f1", -1)]
NRING = 3
SLOT = {name: n % NRING for n, (name, _) in enumerate(RING)}


def previous_use(name, i):
    n = [r[0] for r in RING].index(name)
    back = 0
    while True:
        n -= NRING
        if n < 0:
            n += len(RING)
            back += 1
        who, off = RING[n]
        b = i - back + off
        if i - back < -1:
            return None
        if 0 <= b < NB or (who == "inter" and b == NB):
            return who, off - back


def build(nc, a):
    ctx = ExitStack()
    with ctx:
        def sb(name, shape, dt=F32):
            return ctx.enter_context(nc.sbuf_tensor(name, shape, dt))

        def ps(name, shape):
            return ctx.enter_context(nc.psum_tensor(name, shape, F32))

        def sem(name):
            return ctx.enter_context(nc.semaphore(name))

        X = sb("X", [P, NB, NT, E])
        GATES = sb("GATES", [P, NB, 2, E])
        wmod = sb("wmod", [P, NH, 6 * E])
        cT = sb("cT", [P, NH, NB])
        ctmp = sb("ctmp", [P, 3, NH, NB])
        csilu = sb("csilu", [P, NH, NB])
        modT = sb("modT", [P, 4, NH, NB])
        gates16 = sb("gates16", [NB, 2 * E])
        gstep = sb("gstep", [NB, 2 * E])
        gsign = sb("gsign", [NB, 2 * E])
        gmag = sb("gmag", [NB, 2 * E])
        wqkv = sb("wqkv", [P, NH, 3 * E])
        wo_in = sb("wo_in", [P, NH, E])
        rmsw = sb("rmsw", [P, NH])
        wo = sb("wo", [P, NH, E])
        war = sb("war", [P, NH, NA + NE])
        wbase = sb("wbase", [P, NH, E])
        wb = sb("wb", [P, E])
        dmask = sb("dmask", [P, HG, G, P])
        qdecay = sb("qdecay", [P, H])
        kdecay = sb("kdecay", [P, H])
        rcos = sb("rcos", [P, NT, 8])
        rsin = sb("rsin", [P, NT, 8])
        ident = sb("ident", [P, P])
        diag = sb("diag", [P, HG * D])
        least = sb("least", [P, NE, NE])
        half = sb("half", [P, NT])

        stat1 = sb("stat1", [P, 2, NT, 6])
        mv1 = sb("mv1", [P, 2, NT, 2])
        ve1 = sb("ve1", [P, 2, NT])
        rstd1 = sb("rstd1", [P, 2, NT])
        xn = [sb(f"xn{p}", [P, NT, E]) for p in range(2)]
        hT = [sb(f"hT{p}", [P, NH, NT * P]) for p in range(2)]
        rotc = [sb(f"rotc{t}", [P, 2 * H, 8]) for t in range(NT)]
        rots = [sb(f"rots{t}", [P, 2 * H, 8]) for t in range(NT)]
        qr = [sb(f"qr{t}", [P, H, 2, D]) for t in range(NT)]
        kr = [sb(f"kr{t}", [P, H, D]) for t in range(NT)]
        ks = [sb(f"ks{t}", [P, H, 2, D], F32R) for t in range(NT)]
        kd = [sb(f"kd{p}", [P, H, 2, D]) for p in range(2)]
        v = [sb(f"v{p}", [P, NT, E]) for p in range(2)]
        qhi = [sb(f"qhi{p}", [P, NT, G, P], F32R) for p in range(2)]
        qlo = [sb(f"qlo{p}", [P, NT, G, P], F32R) for p in range(2)]
        kT = [sb(f"kT{p}", [P, NT, G, P], F32R) for p in range(2)]
        state = [sb(f"state{p}", [P, G, HG * D]) for p in range(2)]
        pT = [sb(f"pT{r}", [P, 2, G, P]) for r in range(2)]
        inter = sb("inter", [P, E])
        attn = [sb(f"attn{p}", [P, NT, E]) for p in range(2)]
        sqr = sb("sqr", [P, NT, E])
        ssum = sb("ssum", [P, 2, NT])
        ms = sb("ms", [P, 2, NT])
        rrms = sb("rrms", [P, 2, NT])
        aT = [sb(f"aT{p}", [P, NH, NT * P]) for p in range(2)]
        up = [sb(f"up{p}", [P, NT, E]) for p in range(2)]
        stat2 = sb("stat2", [P, 2, NT, 6])
        mv2 = sb("mv2", [P, 2, NT, 2])
        ve2 = sb("ve2", [P, 2, NT])
        rstd2 = sb("rstd2", [P, 2, NT])
        xm = [sb(f"xm{p}", [P, NT, E]) for p in range(2)]
        h2T = [sb(f"h2T{p}", [P, NH, NT * P]) for p in range(2)]
        lg = sb("lg", [P, 2, NT, NE])
        lmax = sb("lmax", [P, 2, NT])
        lsub = sb("lsub", [P, 2, NT, NE])
        lexp = sb("lexp", [P, 2, NT, NE])
        ldiff = sb("ldiff", [P, NT, NE, NE])
        ahead = sb("ahead", [P, NT, NE, NE])
        rank = sb("rank", [P, 2, NT, NE])
        wsel = sb("wsel", [P, 2, NT, NE])
        wsum = sb("wsum", [P, 2, NT])
        wrec = sb("wrec", [P, 2, NT])
        wexp = sb("wexp", [P, 2, NT, NE])
        z = [sb(f"z{p}", [P, NT, NA]) for p in range(2)]
        zT = [sb(f"zT{p}", [P, NT * P]) for p in range(2)]
        up2 = [sb(f"up2_{p}", [P, NT, E]) for p in range(2)]

        sc_ps = ps("sc_ps", [P, HG, G, P])
        o_ps = ps("o_ps", [P, NT, E])
        ring_ps = ps("ring_ps", [P, NRING, 512])

        def bank(name):
            return ring_ps[:, SLOT[name], :]

        gates_dram = nc.dram_tensor("gates_dram", [NB, 2 * E], F32, kind="Internal").ap()

        S = {n: sem(n) for n in (
            "c_loaded wmod_loaded consts_loaded wqkv_loaded w2_loaded gates_stored gates_loaded0 gates_loaded1 "
            "x_loaded0 x_loaded1 stored "
            "c_exp c_tmp c_silu mod_ps gate_ps mod_done gate_tmp gates_done half_done wo_done "
            "stats1 mean1 ve1_done rstd1_done xn_done t1_ps hT_done qk_ps rotmul rotadd plain_done khi_done ks_done "
            "kd_done v_ps v_done tq_ps tk_ps qhi_done qlo_done kT_done kv_ps state_done sc_ps_done pT_done pv_ps "
            "inter_ps inter_read attn0_done attn1_done sq_done ms_done rrms_done t3_ps aT_done wo_ps up_done "
            "x1_done stats2 mean2 ve2_done rstd2_done xm_done t4_ps h2T_done f1_ps lg_done lmax_done lsub_done "
            "lexp_done ldiff_done ahead_done rank_done wsel_done wsum_done wrec_done wexp_done z_done zT_done f2_ps up2_done "
            "out_done dve_held pool_held").split()}

        last_read = {"inter": ("inter_read", 1, 1), "t1": ("hT_done", 1, 1), "f2": ("up2_done", 1, 1),
                     "t3": ("aT_done", 1, 1), "qk0": ("plain_done", 2, 1), "wo": ("up_done", 1, 1),
                     "qk1": ("plain_done", 2, 2), "v": ("v_done", 1, 1), "tq0": ("qlo_done", 2, 1),
                     "tk0": ("kT_done", 2, 1), "t4": ("h2T_done", 1, 1), "tq1": ("qlo_done", 2, 2),
                     "tk1": ("kT_done", 2, 2), "kv": ("state_done", 1, 1), "f1": ("z_done", 1, 1)}

        x_dram = a["x"].rearrange("b (t p) c -> b p t c", p=P)
        out_dram = a["out"].rearrange("b (t p) c -> b p t c", p=P)

        block = ctx.enter_context(nc.Block())

        @block.sync
        def _(sp):
            sp.dma_start(cT[:], a["cT"].rearrange("(k p) b -> p k b", p=P)).then_inc(S["c_loaded"], 16)
            sp.dma_start(wmod[:], a["wmod"].rearrange("(k p) n -> p k n", p=P)).then_inc(S["wmod_loaded"], 16)

            def load(b):
                if b.first >= 2:
                    sp.wait_ge(S[f"x_loaded{b.parity}"], b.count(8, -8 * b.parity))
                sp.dma_start(X[:, b.at()], x_dram[b.at()].rearrange("o p t c -> p o t c")).then_inc(
                    S[f"x_loaded{b.parity}"], 16)

            load(Batch(0))
            load(Batch(1))
            sp.dma_start(wqkv[:], a["wqkv"].rearrange("(k p) n -> p k n", p=P)).then_inc(S["wqkv_loaded"], 16)
            with sp.Fori(0, NB // 2 - 1) as trip:
                for u in range(2):
                    load(Batch(2 + u, trip))

            def store(b):
                sp.wait_ge(S["out_done"], b.count())
                sp.dma_start(out_dram[b.at()].rearrange("o p t c -> p o t c"), X[:, b.at()]).then_inc(
                    S["stored"], 16)

            with sp.Fori(0, NB // 2) as trip:
                for u in range(2):
                    store(Batch(u, trip))
            sp.wait_ge(S["stored"], 16 * NB)

        @block.tensor
        def _(pe):
            def mm(out, lhsT, rhs, start=True, stop=True):
                return pe.matmul(out, lhsT, rhs, start=start, stop=stop)

            def free_bank(name, i):
                was = previous_use(name, i.first)
                if was:
                    who, off = was
                    s, per, extra = last_read[who]
                    b = i + off
                    if who == "inter" and b.first == NB:
                        s, extra = "zT_done", 0
                    pe.wait_ge(S[s], b.count(per, extra))

            pe.wait_ge(S["c_silu"], 1)
            pe.wait_ge(S["wmod_loaded"], 16)
            for m, part in enumerate((0, 1, 3, 4)):
                for n in range(NH):
                    for k in range(NH):
                        col = part * E + n * P
                        last = mm(ring_ps[:, 0, (m * NH + n) * NB:(m * NH + n + 1) * NB],
                                  wmod[:, k, col:col + P], csilu[:, k, :], k == 0, k == NH - 1)
            last.then_inc(S["mod_ps"], 1)
            for g in range(2):
                for k in range(NH):
                    last = mm(ring_ps[0:NB, 1, g * E:(g + 1) * E], csilu[:, k, :],
                              wmod[:, k, (2 + 3 * g) * E:(3 + 3 * g) * E], k == 0, k == NH - 1)
            last.then_inc(S["gate_ps"], 1)
            pe.wait_ge(S["mod_done"], 2)
            pe.wait_ge(S["gate_tmp"], 3)
            pe.wait_ge(S["consts_loaded"], 16 * 9)
            pe.wait_ge(S["wqkv_loaded"], 16)

            def t1(i):
                b = i + 1
                free_bank("t1", i)
                pe.wait_ge(S["xn_done"], b.count())
                for n in range(NH):
                    for t in range(NT):
                        c = (n * NT + t) * P
                        last = pe.transpose(bank("t1")[:, c:c + P], xn[b.parity][:, t, n * P:(n + 1) * P], ident[:])
                last.then_inc(S["t1_ps"], 1)

            def qk(i, t):
                b = i + 1
                free_bank(f"qk{t}", i)
                pe.wait_ge(S["hT_done"], b.count())
                for n in range(NH):
                    last = mm(bank(f"qk{t}"), hT[b.parity][:, n, t * P:(t + 1) * P], wqkv[:, n, 0:2 * E],
                              n == 0, n == NH - 1)
                last.then_inc(S["qk_ps"], 1)

            def values(i):
                b = i + 1
                free_bank("v", i)
                for t in range(NT):
                    for n in range(NH):
                        last = mm(bank("v")[:, t * E:(t + 1) * E], hT[b.parity][:, n, t * P:(t + 1) * P],
                                  wqkv[:, n, 2 * E:3 * E], n == 0, n == NH - 1)
                last.then_inc(S["v_ps"], 1)

            def t2(i, t):
                b = i + 1
                free_bank(f"tq{t}", i)
                pe.wait_ge(S["rotadd"], b.count(2, t + 1))
                pe.wait_ge(S["plain_done"], b.count(2, t + 1))
                for g in range(G):
                    src = qr[t][:, g * HG:(g + 1) * HG].rearrange("p h c d -> p (h c d)")
                    last = pe.transpose(bank(f"tq{t}")[:, g * P:(g + 1) * P], src, ident[:])
                last.then_inc(S["tq_ps"], 1)
                free_bank(f"tk{t}", i)
                pe.wait_ge(S["ks_done"], b.count(2, t + 1))
                for g in range(G):
                    src = ks[t][:, g * HG:(g + 1) * HG].rearrange("p h c d -> p (h c d)").bitcast(F32)
                    last = pe.transpose(bank(f"tk{t}")[:, g * P:(g + 1) * P], src, ident[:])
                last.then_inc(S["tk_ps"], 1)

            def kv(i):
                b = i + 1
                free_bank("kv", i)
                pe.wait_ge(S["kd_done"], b.count())
                pe.wait_ge(S["v_done"], b.count())
                for g in range(G):
                    lhsT = kd[b.parity][:, g * HG:(g + 1) * HG].rearrange("p h c d -> p (h c d)")
                    last = mm(bank("kv")[:, g * HG * D:(g + 1) * HG * D], lhsT,
                              v[b.parity][:, 0, g * HG * D:(g + 1) * HG * D])
                last.then_inc(S["kv_ps"], 1)

            def scores(b, n):
                c, r = n // 2, n % 2
                if b.first * 4 + n >= 2:
                    pe.wait_ge(S["pT_done"], b.count(4, n - 1))
                pe.wait_ge(S["kT_done"], b.count(2, c + 1))
                pe.wait_ge(S["qlo_done"], b.count(2, c + 1))
                for g in range(G):
                    for q, (first, final) in ((qhi, (True, False)), (qlo, (False, True))):
                        for hh in (2 * r, 2 * r + 1):
                            rows = slice(32 * hh, 32 * hh + 32)
                            last = mm(sc_ps[:, hh, g, :], kT[b.parity][rows, c, g, :], q[b.parity][rows, c, g, :],
                                      first, final)
                last.then_inc(S["sc_ps_done"], 1)

            def pv(b, n):
                c, r = n // 2, n % 2
                pe.wait_ge(S["pT_done"], b.count(4, n + 1))
                if n == 0:
                    pe.wait_ge(S["v_done"], b.count())
                    if b.first > 0:
                        pe.wait_ge(S["attn1_done"], b.count(1, 0))
                for j in range(2):
                    for g in range(G):
                        h = HG * g + 2 * r + j
                        last = mm(o_ps[:, c, h * D:(h + 1) * D], pT[r][:, j, g, :],
                                  v[b.parity][:, c, h * D:(h + 1) * D])
                last.then_inc(S["pv_ps"], 1)

            def inter_and_t5(i):
                bi, bz = i + -1, i + -2
                if not (bi.on or bz.on):
                    return
                free_bank("inter", i)
                if bi.on:
                    pe.wait_ge(S["state_done"], bi.count())
                    for g in range(G):
                        for q, (first, final) in ((qhi, (True, False)), (qlo, (False, True))):
                            last = mm(bank("inter")[:, g * HG * D:(g + 1) * HG * D],
                                      q[bi.parity][:, 1, g, :].bitcast(F32), state[bi.parity][:, g, :], first, final)
                if bz.on:
                    pe.wait_ge(S["z_done"], bz.count())
                    for t in range(NT):
                        last = pe.transpose(bank("inter")[:, E + t * P:E + (t + 1) * P], z[bz.parity][:, t, :], ident[:])
                last.then_inc(S["inter_ps"], 1)

            def t3(i):
                b = i + -1
                free_bank("t3", i)
                pe.wait_ge(S["attn0_done"], b.count())
                pe.wait_ge(S["attn1_done"], b.count())
                for n in range(NH):
                    for t in range(NT):
                        c = (n * NT + t) * P
                        last = pe.transpose(bank("t3")[:, c:c + P], attn[b.parity][:, t, n * P:(n + 1) * P], ident[:])
                last.then_inc(S["t3_ps"], 1)

            def out_proj(i):
                b = i + -1
                free_bank("wo", i)
                pe.wait_ge(S["aT_done"], b.count())
                if b.first == 0:
                    pe.wait_ge(S["wo_done"], NH)
                for t in range(NT):
                    for n in range(NH):
                        last = mm(bank("wo")[:, t * E:(t + 1) * E], aT[b.parity][:, n, t * P:(t + 1) * P], wo[:, n, :],
                                  n == 0, n == NH - 1)
                last.then_inc(S["wo_ps"], 1)

            def t4(i):
                b = i + -1
                free_bank("t4", i)
                pe.wait_ge(S["xm_done"], b.count())
                for n in range(NH):
                    for t in range(NT):
                        c = (n * NT + t) * P
                        last = pe.transpose(bank("t4")[:, c:c + P], xm[b.parity][:, t, n * P:(n + 1) * P], ident[:])
                last.then_inc(S["t4_ps"], 1)

            def f1(i):
                b = i + -1
                free_bank("f1", i)
                pe.wait_ge(S["h2T_done"], b.count())
                if b.first == 0:
                    pe.wait_ge(S["w2_loaded"], 16 * 3)
                for t in range(NT):
                    for n in range(NH):
                        last = mm(bank("f1")[:, t * (NA + NE):(t + 1) * (NA + NE)], h2T[b.parity][:, n, t * P:(t + 1) * P],
                                  war[:, n, :], n == 0, n == NH - 1)
                last.then_inc(S["f1_ps"], 1)

            def f2(i):
                b = i + -2
                free_bank("f2", i)
                pe.wait_ge(S["zT_done"], b.count())
                for t in range(NT):
                    out = bank("f2")[:, t * E:(t + 1) * E]
                    for n in range(NH):
                        mm(out, h2T[b.parity][:, n, t * P:(t + 1) * P], wbase[:, n, :], n == 0, False)
                    last = mm(out, zT[b.parity][:, t * P:(t + 1) * P], wb[:], False, True)
                last.then_inc(S["f2_ps"], 1)

            def iteration(i):
                front, mid, back, tail = i + 1, i, i + -1, i + -2
                if mid.on:
                    scores(mid, 0)
                inter_and_t5(i)
                if back.on:
                    pv(back, 3)
                if front.on:
                    t1(i)
                if tail.on:
                    f2(i)
                if mid.on:
                    scores(mid, 1)
                if back.on:
                    t3(i)
                if mid.on:
                    pv(mid, 0)
                if front.on:
                    qk(i, 0)
                if back.on:
                    out_proj(i)
                if front.on:
                    qk(i, 1)
                if mid.on:
                    scores(mid, 2)
                if front.on:
                    values(i)
                if mid.on:
                    pv(mid, 1)
                if front.on:
                    t2(i, 0)
                if back.on:
                    t4(i)
                if front.on:
                    t2(i, 1)
                    kv(i)
                if back.on:
                    f1(i)
                if mid.on:
                    scores(mid, 3)
                    pv(mid, 2)

            pipeline(pe, iteration, -1, NB + 1)

        @block.scalar
        def _(act):
            loads = (("qdecay", qdecay), ("kdecay", kdecay), ("rcos", rcos), ("rsin", rsin), ("ident", ident),
                     ("diag", diag), ("dmask", dmask), ("least", least))
            for name, dst in loads:
                act.dma_start(dst[:], a[name]).then_inc(S["consts_loaded"], 16)
            act.dma_start(rmsw[:], a["rms_w"]).then_inc(S["consts_loaded"], 16)
            act.wait_ge(S["c_loaded"], 16)
            act.activation(ctmp[:, 0], cT[:], ACT.Exp, scale=-1.0).then_inc(S["c_exp"], 1)
            act.wait_ge(S["mod_done"], 2)

            def h_evac(b, src, dst, shift, scale, ready, done):
                act.wait_ge(S[ready], b.count())
                for n in range(NH):
                    k = b.at()
                    last = act.activation(dst[:, n, :], src[:, n * NT * P:(n + 1) * NT * P], ACT.Identity,
                                          bias=modT[:, shift, n, k], scale=modT[:, scale, n, k])
                last.then_inc(S[done], 1)

            def plain_dims(i, t):
                b = i + 1
                qkv = bank(f"qk{t}").rearrange("p (w h d) -> p w h d", w=2, d=D)
                act.wait_ge(S["rotmul"], b.count(2, t + 1))
                act.activation(kr[t][:, :, 8:16], qkv[:, 1, :, 8:16], ACT.Copy)
                act.activation(qr[t][:, :, :, 8:16], qkv[:, 0, :, 8:16].unsqueeze(2).broadcast_to([P, H, 2, 8]),
                               ACT.Copy).then_inc(S["plain_done"], 1)

            def iteration(i):
                front, mid, back, tail = i + 1, i, i + -1, i + -2
                if tail.on:
                    act.wait_ge(S["inter_ps"], tail.count(1, 2))
                    act.activation(zT[tail.parity][:], bank("inter")[:, E:2 * E], ACT.Copy).then_inc(S["zT_done"], 1)
                if front.on:
                    h_evac(front, bank("t1"), hT[front.parity], SA, CA, "t1_ps", "hT_done")
                if back.on:
                    act.wait_ge(S["pv_ps"], back.count(4, 4))
                    act.activation(attn[back.parity][:, 0, :], o_ps[:, 0, :], ACT.Copy).then_inc(S["attn0_done"], 1)
                    act.wait_ge(S["attn0_done"], back.count())
                    act.activation(sqr[:, 0], attn[back.parity][:, 0, :], ACT.Square,
                                   accum_out=ssum[:, back.parity, 0:1])
                    act.wait_ge(S["attn1_done"], back.count())
                    act.activation(sqr[:, 1], attn[back.parity][:, 1, :], ACT.Square,
                                   accum_out=ssum[:, back.parity, 1:2]).then_inc(S["sq_done"], 1)
                    act.wait_ge(S["t3_ps"], back.count())
                    act.activation(aT[back.parity][:], bank("t3").rearrange("p (n c) -> p n c", n=NH),
                                   ACT.Copy).then_inc(S["aT_done"], 1)
                if front.on:
                    plain_dims(i, 0)
                    plain_dims(i, 1)
                    act.wait_ge(S["v_ps"], front.count())
                    act.activation(v[front.parity][:], bank("v").rearrange("p (t c) -> p t c", t=NT),
                                   ACT.Copy).then_inc(S["v_done"], 1)

                def qk_evac(t):
                    act.wait_ge(S["tq_ps"], front.count(2, t + 1))
                    act.activation(qhi[front.parity][:, t], bank(f"tq{t}").rearrange("p (g c) -> p g c", g=G),
                                   ACT.Copy).then_inc(S["qhi_done"], 1)
                    act.wait_ge(S["tk_ps"], front.count(2, t + 1))
                    act.activation(kT[front.parity][:, t], bank(f"tk{t}").rearrange("p (g c) -> p g c", g=G),
                                   ACT.Copy).then_inc(S["kT_done"], 1)

                if front.on:
                    qk_evac(0)
                if back.on:
                    h_evac(back, bank("t4"), h2T[back.parity], SB, CB, "t4_ps", "h2T_done")
                if front.on:
                    qk_evac(1)
                if back.on:
                    act.wait_ge(S["f1_ps"], back.count())
                    logits = bank("f1")[:, 0:NT * (NA + NE)].rearrange("p (t c) -> p t c", t=NT)[:, :, NA:NA + NE]
                    act.activation(lg[:, back.parity], logits, ACT.Copy).then_inc(S["lg_done"], 1)
                    act.wait_ge(S["lsub_done"], back.count())
                    act.activation(lexp[:, back.parity], lsub[:, back.parity], ACT.Exp).then_inc(S["lexp_done"], 1)

            pipeline(act, iteration, -1, NB + 1)

        @block.gpsimd
        def _(pool):
            pool.dma_start(wo_in[:], a["wo"].rearrange("(k p) n -> p k n", p=P)).then_inc(S["w2_loaded"], 16)
            pool.dma_start(war[:], a["war"].rearrange("(k p) n -> p k n", p=P)).then_inc(S["w2_loaded"], 16)
            pool.dma_start(wbase[:], a["wbase"].rearrange("(k p) n -> p k n", p=P)).then_inc(S["w2_loaded"], 16)
            pool.dma_start(wb[:], a["wb"]).then_inc(S["w2_loaded"], 16)
            for p in range(2):
                pool.memset(kd[p][:], 0.0)
            pool.memset(half[:], -0.5).then_inc(S["half_done"], 1)
            pool.wait_ge(S["w2_loaded"], 16 * 4)
            pool.wait_ge(S["consts_loaded"], 16 * 9)
            for n in range(NH):
                pool.tensor_scalar(wo[:, n, :], wo_in[:, n, :], rmsw[:, n:n + 1], None, ALU.mult).then_inc(
                    S["wo_done"], 1)
            pool.wait_ge(S["half_done"], 1)
            pool.wait_ge(S["gates_done"], 1)
            pool.dma_start(gates_dram, gates16[:]).then_inc(S["gates_stored"], 16)
            pool.wait_ge(S["gates_stored"], 16)
            gsrc = gates_dram.rearrange("b n -> (b n)").partition_broadcast(P).rearrange(
                "p (b g c) -> p b g c", b=NB, g=2)
            pool.dma_start(GATES[:, 0:4], gsrc[:, 0:4]).then_inc(S["gates_loaded0"], 16)
            pool.dma_start(GATES[:, 4:NB], gsrc[:, 4:NB]).then_inc(S["gates_loaded1"], 16)

            def rsqrt(b, var, mul, tmp, out, ready, mid_sem, done):
                hold(pool, S[ready], b.count(), S["pool_held"])
                pool.tensor_scalar(tmp, var, mul, EPS, ALU.mult, ALU.add).then_inc(S[mid_sem], 1)
                pool.wait_ge(S[mid_sem], b.count())
                pool.tensor_tensor(out, tmp, half[:], ALU.pow).then_inc(S[done], 1)

            def rotate(i, t):
                b = i + 1
                pool.wait_ge(S["rotmul"], b.count(2, t + 1))
                pool.tensor_tensor(kr[t][:, :, 0:8], rotc[t][:, H:2 * H, :], rots[t][:, H:2 * H, :], ALU.add)
                pool.tensor_tensor(qr[t][:, :, :, 0:8], rotc[t][:, 0:H, :].unsqueeze(2).broadcast_to([P, H, 2, 8]),
                                   rots[t][:, 0:H, :].unsqueeze(2).broadcast_to([P, H, 2, 8]),
                                   ALU.add).then_inc(S["rotadd"], 1)
                pool.wait_ge(S["rotadd"], b.count(2, t + 1))
                hold(pool, S["plain_done"], b.count(2, t + 1), S["pool_held"])
                pool.tensor_copy(ks[t][:, :, 0, :], kr[t][:]).then_inc(S["khi_done"], 1)
                pool.wait_ge(S["khi_done"], b.count(2, t + 1))
                pool.tensor_tensor(ks[t][:, :, 1, :], kr[t][:], ks[t][:, :, 0, :].bitcast(F32),
                                   ALU.subtract).then_inc(S["ks_done"], 1)
                if t == 0:
                    pool.tensor_tensor(kd[b.parity][:, :, 0, :], kr[0][:], kdecay[:].unsqueeze(2).broadcast_to([P, H, D]),
                                       ALU.mult).then_inc(S["kd_done"], 1)

            def iteration(i):
                front, back, tail, ahead_b = i + 1, i + -1, i + -2, i + 2
                if tail.on:
                    hold(pool, S["up2_done"], tail.count(), S["pool_held"])
                    pool.tensor_tensor(X[:, tail.at()], X[:, tail.at()], up2[tail.parity][:].unsqueeze(1),
                                       ALU.add).then_inc(S["out_done"], 1)
                if back.on:
                    p = back.parity
                    rsqrt(back, ssum[:, p], 1.0 / E, ms[:, p], rrms[:, p], "sq_done", "ms_done", "rrms_done")
                if front.on:
                    rotate(i, 0)
                if back.on:
                    hold(pool, S["up_done"], back.count(), S["pool_held"])
                    pool.tensor_tensor(X[:, back.at()], X[:, back.at()], up[back.parity][:].unsqueeze(1),
                                       ALU.add).then_inc(S["x1_done"], 1)
                if front.on:
                    rotate(i, 1)
                if back.on:
                    rsqrt(back, mv2[:, p, :, 1], 1.0, ve2[:, p], rstd2[:, p], "mean2", "ve2_done", "rstd2_done")
                    pool.wait_ge(S["lg_done"], back.count())
                    if back.first > 0:
                        pool.wait_ge(S["ahead_done"], back.count(1, 0))
                    pool.tensor_tensor(ldiff[:], lg[:, p].unsqueeze(2).broadcast_to([P, NT, NE, NE]),
                                       lg[:, p].unsqueeze(3).broadcast_to([P, NT, NE, NE]),
                                       ALU.subtract).then_inc(S["ldiff_done"], 1)
                if ahead_b.on:
                    q = ahead_b.parity
                    rsqrt(ahead_b, mv1[:, q, :, 1], 1.0, ve1[:, q], rstd1[:, q], "mean1", "ve1_done", "rstd1_done")

            pipeline(pool, iteration, -2, NB + 1)

        @block.vector
        def _(dve):
            dve.wait_ge(S["c_exp"], 1)
            dve.tensor_scalar(ctmp[:, 1], ctmp[:, 0], 1.0, None, ALU.add).then_inc(S["c_tmp"], 1)
            dve.wait_ge(S["c_tmp"], 1)
            dve.reciprocal(ctmp[:, 2], ctmp[:, 1]).then_inc(S["c_tmp"], 1)
            dve.wait_ge(S["c_tmp"], 2)
            dve.tensor_tensor(csilu[:], cT[:], ctmp[:, 2], ALU.mult).then_inc(S["c_silu"], 1)
            dve.wait_ge(S["mod_ps"], 1)
            mods = ring_ps[:, 0, 0:4 * NH * NB].rearrange("p (m n b) -> p m n b", m=4, n=NH)
            for first, plus in ((SA, 0.0), (CA, 1.0)):
                ins = dve.tensor_scalar(modT[:, first::2], mods[:, first::2], plus, None, ALU.add)
                ins.then_inc(S["mod_done"], 1)
            dve.wait_ge(S["gate_ps"], 1)
            gps = ring_ps[0:NB, 1, :]
            dve.tensor_scalar(gstep[:], gps, 0.0, 2.0, ALU.is_ge, ALU.mult).then_inc(S["gate_tmp"], 1)
            dve.wait_ge(S["gate_tmp"], 1)
            dve.tensor_scalar(gsign[:], gstep[:], -1.0, None, ALU.add).then_inc(S["gate_tmp"], 1)
            dve.wait_ge(S["gate_tmp"], 2)
            dve.tensor_tensor(gmag[:], gps, gsign[:], ALU.mult).then_inc(S["gate_tmp"], 1)
            dve.wait_ge(S["gate_tmp"], 3)
            dve.scalar_tensor_tensor(out=gates16[:], in0=gmag[:], scalar=0.25, in1=gsign[:], op0=ALU.max,
                                     op1=ALU.mult).then_inc(S["gates_done"], 1)

            def stats(x, st, mv, b, stats_sem, mean_sem):
                for t in range(NT):
                    last = dve.bn_stats(st[:, b.parity, t, :], x[:, t, :])
                last.then_inc(S[stats_sem], 1)
                hold(dve, S[stats_sem], b.count(), S["dve_held"])
                for t in range(NT):
                    last = dve.bn_aggr(mv[:, b.parity, t, :], st[:, b.parity, t, :])
                last.then_inc(S[mean_sem], 1)

            def normalise(x, dst, mv, rstd, b):
                for t in range(NT):
                    last = dve.tensor_scalar(dst[:, t, :], x[:, t, :], mv[:, b.parity, t, 0:1],
                                             rstd[:, b.parity, t:t + 1], ALU.subtract, ALU.mult)
                return last

            def x_of(b):
                return X[:, b.at()].rearrange("p o t c -> p (o t) c")

            def mask(b, n):
                c, r = n // 2, n % 2
                dve.wait_ge(S["sc_ps_done"], b.count(4, n + 1))
                if b.first * 4 + n >= 2:
                    dve.wait_ge(S["pv_ps"], b.count(4, n - 1))
                dve.tensor_tensor(pT[r][:], sc_ps[:, 2 * r:2 * r + 2], dmask[:, 2 * r:2 * r + 2],
                                  ALU.mult).then_inc(S["pT_done"], 1)

            def rot(i, t):
                b = i + 1
                dve.wait_ge(S["qk_ps"], b.count(2, t + 1))
                if b.first > 0:
                    dve.wait_ge(S["rotadd"], b.count(2, t - 1))
                qkv = bank(f"qk{t}").rearrange("p (h d) -> p h d", d=D)
                dve.tensor_tensor(rotc[t][:], qkv[:, :, 0:8], rcos[:, t].unsqueeze(1).broadcast_to([P, 2 * H, 8]),
                                  ALU.mult)
                dve.tensor_tensor(rots[t][:, :, 0:4], qkv[:, :, 4:8],
                                  rsin[:, t, 0:4].unsqueeze(1).broadcast_to([P, 2 * H, 4]), ALU.mult)
                dve.tensor_tensor(rots[t][:, :, 4:8], qkv[:, :, 0:4],
                                  rsin[:, t, 4:8].unsqueeze(1).broadcast_to([P, 2 * H, 4]),
                                  ALU.mult).then_inc(S["rotmul"], 1)

            def q_low(i, t):
                b = i + 1
                p = b.parity
                dve.wait_ge(S["qhi_done"], b.count(2, t + 1))
                dve.tensor_tensor(qlo[p][:, t], bank(f"tq{t}").rearrange("p (g c) -> p g c", g=G),
                                  qhi[p][:, t].bitcast(F32), ALU.subtract).then_inc(S["qlo_done"], 1)

            def ln1_stats(i):
                b = i + 2
                dve.wait_ge(S[f"x_loaded{b.parity}"], b.count(8, 16 - 8 * b.parity))
                stats(x_of(b), stat1, mv1, b, "stats1", "mean1")

            def ln1_apply(i):
                b = i + 2
                dve.wait_ge(S["rstd1_done"], b.count())
                if b.first >= 2:
                    dve.wait_ge(S["t1_ps"], b.count(1, -1))
                normalise(x_of(b), xn[b.parity], mv1, rstd1, b).then_inc(S["xn_done"], 1)

            dve.wait_ge(S["consts_loaded"], 16 * 9)

            def iteration(i):
                front, mid, back, tail = i + 1, i, i + -1, i + -2
                pb = back.parity
                if mid.on:
                    mask(mid, 0)
                if back.on:
                    dve.wait_ge(S["inter_ps"], back.count())
                    if tail.on:
                        dve.wait_ge(S["zT_done"], tail.count())
                    dve.tensor_tensor(inter[:].rearrange("p (h d) -> p h d", d=D),
                                      bank("inter")[:, 0:E].rearrange("p (h d) -> p h d", d=D),
                                      qdecay[:].unsqueeze(2).broadcast_to([P, H, D]),
                                      ALU.mult).then_inc(S["inter_read"], 1)
                    dve.wait_ge(S["inter_read"], back.count())
                    dve.wait_ge(S["attn0_done"], back.count())
                    dve.tensor_tensor(attn[pb][:, 1, :], o_ps[:, 1, :], inter[:], ALU.add).then_inc(
                        S["attn1_done"], 1)
                if tail.on:
                    dve.wait_ge(S["f2_ps"], tail.count())
                    gb = GATES[:, tail.at(), 1, :].broadcast_to([P, NT, E])
                    dve.tensor_tensor(up2[tail.parity][:], bank("f2").rearrange("p (t c) -> p t c", t=NT), gb,
                                      ALU.mult).then_inc(S["up2_done"], 1)
                if mid.on:
                    mask(mid, 1)
                if front.on:
                    rot(i, 0)
                if back.on:
                    if back.first == 0:
                        dve.wait_ge(S["gates_loaded0"], 16)
                    if i.first == LOOP_FIRST - 1:
                        dve.wait_ge(S["gates_loaded1"], 16)
                    dve.wait_ge(S["wo_ps"], back.count())
                    dve.wait_ge(S["rrms_done"], back.count())
                    for t in range(NT):
                        last = dve.scalar_tensor_tensor(
                            out=up[pb][:, t, :], in0=bank("wo")[:, t * E:(t + 1) * E], scalar=rrms[:, pb, t:t + 1],
                            in1=GATES[:, back.at(), 0, :].rearrange("p o c -> p (o c)"), op0=ALU.mult, op1=ALU.mult)
                    last.then_inc(S["up_done"], 1)
                if front.on:
                    rot(i, 1)
                if mid.on:
                    mask(mid, 2)
                if back.on:
                    dve.wait_ge(S["x1_done"], back.count())
                    stats(x_of(back), stat2, mv2, back, "stats2", "mean2")
                if front.on:
                    q_low(i, 0)
                if back.on:
                    dve.wait_ge(S["rstd2_done"], back.count())
                    normalise(x_of(back), xm[pb], mv2, rstd2, back).then_inc(S["xm_done"], 1)
                if front.on:
                    q_low(i, 1)
                    dve.wait_ge(S["kv_ps"], front.count())
                    dve.tensor_tensor(state[front.parity][:], bank("kv")[:, 0:E].rearrange("p (g c) -> p g c", g=G),
                                      diag[:].unsqueeze(1).broadcast_to([P, G, HG * D]),
                                      ALU.mult).then_inc(S["state_done"], 1)
                if back.on:
                    dve.wait_ge(S["lg_done"], back.count())
                    dve.reduce_max(lmax[:, pb], lg[:, pb], AX_X).then_inc(S["lmax_done"], 1)
                    dve.wait_ge(S["lmax_done"], back.count())
                    dve.tensor_tensor(lsub[:, pb], lg[:, pb], lmax[:, pb].unsqueeze(2).broadcast_to([P, NT, NE]),
                                      ALU.subtract).then_inc(S["lsub_done"], 1)
                if mid.on:
                    mask(mid, 3)
                if (i + 2).on:
                    ln1_stats(i)
                if back.on:
                    dve.wait_ge(S["ldiff_done"], back.count())
                    dve.tensor_tensor(ahead[:], ldiff[:], least[:].unsqueeze(1).broadcast_to([P, NT, NE, NE]),
                                      ALU.is_ge).then_inc(S["ahead_done"], 1)
                    dve.wait_ge(S["ahead_done"], back.count())
                    dve.reduce_sum(rank[:, pb], ahead[:], AX_X).then_inc(S["rank_done"], 1)
                    dve.wait_ge(S["rank_done"], back.count())
                    dve.wait_ge(S["lexp_done"], back.count())
                    dve.scalar_tensor_tensor(out=wsel[:, pb], in0=rank[:, pb], scalar=2.0, in1=lexp[:, pb],
                                             op0=ALU.is_lt, op1=ALU.mult).then_inc(S["wsel_done"], 1)
                    dve.wait_ge(S["wsel_done"], back.count())
                    dve.reduce_sum(wsum[:, pb], wsel[:, pb], AX_X).then_inc(S["wsum_done"], 1)
                    dve.wait_ge(S["wsum_done"], back.count())
                    dve.reciprocal(wrec[:, pb], wsum[:, pb]).then_inc(S["wrec_done"], 1)
                    dve.wait_ge(S["wrec_done"], back.count())
                    dve.scalar_tensor_tensor(out=wexp[:, pb], in0=wsel[:, pb], scalar=SCALING,
                                             in1=wrec[:, pb].unsqueeze(2).broadcast_to([P, NT, NE]),
                                             op0=ALU.mult, op1=ALU.mult).then_inc(S["wexp_done"], 1)
                    dve.wait_ge(S["wexp_done"], back.count())
                    lora = bank("f1")[:, 0:NT * (NA + NE)].rearrange("p (t c) -> p t c", t=NT)[:, :, 0:NA]
                    dve.tensor_tensor(z[pb][:].rearrange("p t (e r) -> p t e r", r=R),
                                      lora.rearrange("p t (e r) -> p t e r", r=R),
                                      wexp[:, pb].unsqueeze(3).broadcast_to([P, NT, NE, R]),
                                      ALU.mult).then_inc(S["z_done"], 1)
                if (i + 2).on:
                    ln1_apply(i)

            pipeline(dve, iteration, -2, NB + 1)


def shape_tables():
    import math

    import numpy as np

    f = np.float32
    start = 2.0 ** (-2.0 ** (-(math.log2(H) - 3)))
    slopes = np.array([start * start ** i for i in range(H)], dtype=f)
    r = np.exp(-slopes.astype(np.float64)).astype(f).astype(np.float64)
    i = np.arange(P, dtype=np.float64)
    diff = i[None, :] - i[:, None]
    decay = np.where(diff[None] >= 0, r[:, None, None] ** np.maximum(diff, 0)[None], 0.0)
    dmask = decay.reshape(G, HG, P, P).transpose(2, 1, 0, 3)
    freq = np.concatenate([(f(1.0 / 1024.0) ** np.linspace(0.0, 1.0, D // 4, dtype=f)).astype(f)])
    theta = (np.arange(NT * P, dtype=f)[:, None] * freq[None, :]).astype(f).astype(np.float64)
    cos, sin = np.cos(theta), np.sin(theta)
    rcos = np.concatenate([cos, cos], axis=1).reshape(NT, P, 8).transpose(1, 0, 2)
    rsin = np.concatenate([sin, -sin], axis=1).reshape(NT, P, 8).transpose(1, 0, 2)
    row, col = np.arange(P)[:, None], np.arange(HG * D)[None, :]
    diag = (row // 32 == col // D) & (row % 32 < D)
    e = np.arange(NE)
    ej = e[None, :] - e[:, None]
    least = np.broadcast_to(np.where(ej < 0, 0.0, np.where(ej > 0, np.finfo(f).tiny, np.finfo(f).max)), (P, NE, NE))
    return {k: np.ascontiguousarray(t, dtype=f) for k, t in {
        "dmask": dmask, "qdecay": (r[:, None] ** (i[None] + 1.0)).T, "kdecay": (r[:, None] ** (P - 1.0 - i[None])).T,
        "rcos": rcos, "rsin": rsin, "ident": np.eye(P), "diag": diag, "least": least}.items()}


def kernel(**inputs):
    import numpy as np
    import concourse.bacc as bacc
    from concourse.bass_utils import run_bass_kernel_spmd as run

    f = {k[3:]: np.asarray(t) for k, t in inputs.items()}
    order = np.concatenate([np.r_[0:4, 8:12, 4:8, 12:16] + D * h for h in range(H)])
    arrays = {
        "x": f["attn_x"], "cT": f["c"].T, "wmod": f["wmod"],
        "wqkv": np.concatenate([f["attn_Wq"][:, order], f["attn_Wk"][:, order], f["attn_Wv"]], axis=1),
        "wo": f["attn_Wo"], "rms_w": f["attn_rms_w"].reshape(NH, P).T,
        "war": np.concatenate([f["ffn_lora_A"].reshape(NA, E).T, f["ffn_router_w"].T], axis=1),
        "wbase": f["ffn_weight"].T, "wb": f["ffn_lora_B"].transpose(0, 2, 1).reshape(NA, E),
    }
    arrays.update(shape_tables())
    arrays = {f"in_{k}": np.ascontiguousarray(t) for k, t in arrays.items()}
    nc = bacc.Bacc("TRN2", target_bir_lowering=False, num_devices=1)
    a = {k[3:]: nc.dram_tensor(k, t.shape, mybir.dt.from_np(t.dtype), kind="ExternalInput").ap()
         for k, t in arrays.items()}
    a["out"] = nc.dram_tensor("out_0", (NB, NT * P, E), F32, kind="ExternalOutput").ap()
    build(nc, a)
    r = run(nc, [arrays], core_ids=[0])
    return r.results[0]["out_0"]
```

```python
from contextlib import ExitStack

import concourse.bass as bass
from concourse import mybir

F32 = mybir.dt.float32
F32R = mybir.dt.float32r
ALU = mybir.AluOpType
ACT = mybir.ActivationFunctionType
AX_X = mybir.AxisListType.X

P = 128
NB = 16
NT = 2
E = 256
NH = E // P
H = 16
D = E // H
G = 4
HG = H // G
NE = 8
R = 16
NA = NE * R
EPS = 1e-5
SCALING = 2.0
SA, CA, SB, CB = range(4)


class Batch:

    def __init__(self, first, trip=None):
        self.first, self.trip = first, trip

    def __add__(self, k):
        return Batch(self.first + k, self.trip)

    @property
    def on(self):
        return 0 <= self.first < NB

    @property
    def parity(self):
        return self.first % 2

    def count(self, per=1, extra=1):
        at = per * self.first + extra
        return at if self.trip is None else self.trip * (2 * per) + at

    def at(self):
        return bass.ds(self.count(1, 0), 1)


LOOP_FIRST, LOOP_TRIPS = 3, 5


def pipeline(eng, iteration, first, last):
    for i in range(first, LOOP_FIRST):
        iteration(Batch(i))
    with eng.Fori(0, LOOP_TRIPS) as trip:
        for u in range(2):
            iteration(Batch(LOOP_FIRST + u, trip))
    for i in range(LOOP_FIRST + 2 * LOOP_TRIPS, last + 1):
        iteration(Batch(i))


def hold(eng, semaphore, value, held):
    eng.wait_ge(semaphore, value)
    eng.sem_inc(held, 1)


RING = [("ss", -1), ("t1", 2), ("wo", -1), ("t5", -2), ("qk0", 1), ("qk1", 1), ("f2", -2), ("v", 1), ("t4", -1),
        ("tk0", 1), ("tq0", 1), ("f1", -1), ("tk1", 1), ("tq1", 1), ("kv", 1)]
NRING = 3
SLOT = {name: n % NRING for n, (name, _) in enumerate(RING)}


def previous_use(name, i):
    n = [r[0] for r in RING].index(name)
    back = 0
    while True:
        n -= NRING
        if n < 0:
            n += len(RING)
            back += 1
        who, off = RING[n]
        b = i - back + off
        if i - back < -2:
            return None
        if 0 <= b < NB:
            return who, off - back


def build(nc, a):
    ctx = ExitStack()
    with ctx:
        def sb(name, shape, dt=F32):
            return ctx.enter_context(nc.sbuf_tensor(name, shape, dt))

        def ps(name, shape):
            return ctx.enter_context(nc.psum_tensor(name, shape, F32))

        def sem(name):
            return ctx.enter_context(nc.semaphore(name))

        X = sb("X", [P, NB, NT, E])
        scratch = sb("scratch", [P, NH * 6 * E])
        wmod = scratch[:].rearrange("p (k n) -> p k n", k=NH)
        xn, xm, up = ([scratch[:, (2 * w + p) * NT * E:(2 * w + p + 1) * NT * E].rearrange("p (t c) -> p t c", t=NT)
                       for p in range(2)] for w in range(3))
        cT = sb("cT", [P, NH, NB])
        ctmp = sb("ctmp", [P, 3, NH, NB])
        csilu = sb("csilu", [P, NH, NB])
        modT = sb("modT", [P, 4, NH, NB])
        gstep, gsign, gmag, gates16 = (scratch[0:NB, (2 + n) * NT * E:(3 + n) * NT * E] for n in range(4))
        scratch2 = sb("scratch2", [P, 5 * NT * E])
        wqkv = scratch2[:, 0:6 * E].rearrange("p (k n) -> p k n", k=NH)
        wo_in = scratch2[:, 6 * E:8 * E].rearrange("p (k n) -> p k n", k=NH)
        wbase = scratch2[:, 8 * E:10 * E].rearrange("p (k n) -> p k n", k=NH)
        sqr = [scratch2[:, 2 * p * E:2 * (p + 1) * E].rearrange("p (n t) -> p n t", n=NH) for p in range(2)]
        up2 = [scratch2[:, (4 + 2 * p) * E:(6 + 2 * p) * E].rearrange("p (t c) -> p t c", t=NT) for p in range(2)]
        z = [scratch2[:, (8 + p) * E:(9 + p) * E].rearrange("p (t c) -> p t c", t=NT) for p in range(2)]
        rmsw = sb("rmsw", [P, NH])
        wo = sb("wo", [P, NH, E])
        wqkv_s = [sb(f"wqkv_{x}", [P, NH, 3 * E], F32R) for x in ("hi", "lo")]
        wo_s = [sb(f"wo_{x}", [P, NH, E], F32R) for x in ("hi", "lo")]
        wbase_s = [sb(f"wbase_{x}", [P, NH, E], F32R) for x in ("hi", "lo")]
        wb_s = [sb(f"wb_{x}", [P, E], F32R) for x in ("hi", "lo")]
        war = sb("war", [P, NH, NA + NE])
        wb = sb("wb", [P, E])
        dmask = sb("dmask", [P, 2, 2, 2, 2, P])
        qdecay = sb("qdecay", [P, H])
        kdecay = sb("kdecay", [P, H])
        rcos = sb("rcos", [P, NT, 8])
        rsin = sb("rsin", [P, NT, 8])
        ident = sb("ident", [P, P])
        diag = sb("diag", [P, P])
        even_odd = sb("even_odd", [P, 2])
        ones = sb("ones", [P, 1])
        least = sb("least", [P, NE, NE])
        half = sb("half", [P, NT])

        stat1 = sb("stat1", [P, 2, NT, 6])
        mv1 = sb("mv1", [P, 2, NT, 2])
        ve1 = sb("ve1", [P, 2, NT])
        rstd1 = sb("rstd1", [P, 2, NT])
        gate = [sb(f"gate{p}", [P, 2, E]) for p in range(2)]
        hT = sb("hT", [P, NH, NT * P])
        hT_s = [[sb(f"hT{x}{p}", [P, NH, NT * P], F32R) for x in ("hi", "lo")] for p in range(2)]
        rotc = [sb(f"rotc{t}", [P, 2 * H, 8]) for t in range(NT)]
        rots = [sb(f"rots{t}", [P, 2 * H, 8]) for t in range(NT)]
        qr = [sb(f"qr{t}", [P, H, 2, D]) for t in range(NT)]
        kr = [sb(f"kr{t}", [P, H, D]) for t in range(NT)]
        ks = [sb(f"ks{t}", [P, H, 2, D], F32R) for t in range(NT)]
        kd = [sb(f"kd{p}", [P, H, D]) for p in range(2)]
        qd = [sb(f"qd{p}", [P, H, D]) for p in range(2)]
        qdT = [sb(f"qdT{p}", [P, NH, P]) for p in range(2)]
        v = [sb(f"v{p}", [P, NT, H // 2, 3 * D]) for p in range(2)]
        q_s = [[sb(f"q{x}{p}", [P, NT, G, 2, P], F32R) for x in ("hi", "lo")] for p in range(2)]
        kT = [sb(f"kT{p}", [P, NT, G, P], F32R) for p in range(2)]
        state = [sb(f"state{p}", [P, NH, P]) for p in range(2)]
        pT = [sb(f"pT{r}", [P, 2, 2, 2, P]) for r in range(2)]
        ms = sb("ms", [P, 2, NT])
        rrms = sb("rrms", [P, 2, NT])
        aT_s = [[sb(f"aT{x}{p}", [P, NH, NT * P], F32R) for x in ("hi", "lo")] for p in range(2)]
        stat2 = sb("stat2", [P, 2, NT, 6])
        mv2 = sb("mv2", [P, 2, NT, 2])
        ve2 = sb("ve2", [P, 2, NT])
        rstd2 = sb("rstd2", [P, 2, NT])
        h2T = sb("h2T", [P, NH, NT * P])
        h2T_s = [[sb(f"h2T{x}{p}", [P, NH, NT * P], F32R) for x in ("hi", "lo")] for p in range(2)]
        f1s = sb("f1s", [P, 2, NT, NA + NE])
        lg = f1s[:, :, :, NA:NA + NE]
        lmax = sb("lmax", [P, 2, NT])
        lsub = sb("lsub", [P, 2, NT, NE])
        lexp = sb("lexp", [P, 2, NT, NE])
        ldiff = sb("ldiff", [P, NT, NE, NE])
        ahead = sb("ahead", [P, NT, NE, NE])
        rank = sb("rank", [P, 2, NT, NE])
        wsel = sb("wsel", [P, 2, NT, NE])
        wsum = sb("wsum", [P, 2, NT])
        wrec = sb("wrec", [P, 2, NT])
        wexp = sb("wexp", [P, 2, NT, NE])
        zT_s = [[sb(f"zT{x}{p}", [P, NT * P], F32R) for x in ("hi", "lo")] for p in range(2)]

        sc_ps = ps("sc_ps", [P, 4, 2, 2, P])
        o_ps = ps("o_ps", [P, NH, NT * P])
        ring_ps = ps("ring_ps", [P, NRING, 512])

        def bank(name):
            return ring_ps[:, SLOT[name], :]

        gates_dram = nc.dram_tensor("gates_dram", [NB, 2 * E], F32, kind="Internal").ap()

        S = {n: sem(n) for n in (
            "c_loaded wmod_loaded consts_loaded wqkv_loaded w2_loaded gates_stored gate_loaded0 gate_loaded1 "
            "x_loaded0 x_loaded1 stored "
            "c_exp c_tmp c_silu mod_ps gate_ps mod_done gate_tmp gates_done const_done wo_scaled w_hi w_lo "
            "stats1 mean1 ve1_done rstd1_done xn_done t1_ps hT_done hT_split qk_ps rotmul rotadd plain_done khi_done "
            "ks_done kd_done qd_done v_ps v_done tq_ps tk_ps qhi_done qlo_done kT_done kv_ps qdT_done state_done "
            "sc_done pT_done pv_done o_copied aT_done ss_ps ms_done rrms_done wo_ps up_done x1_done stats2 mean2 "
            "ve2_done rstd2_done xm_done t4_ps h2T_done h2T_split f1_ps lg_done lmax_done lsub_done lexp_done "
            "ldiff_done ahead_done rank_done wsel_done wsum_done wrec_done wexp_done z_done t5_ps zhi_done zlo_done "
            "f2_ps up2_done out_done dve_held pool_held").split()}

        last_read = {"t5": ("zlo_done", 1, 1), "t1": ("hT_done", 1, 1), "f2": ("up2_done", 1, 1),
                     "ss": ("ms_done", 1, 1), "qk0": ("plain_done", 2, 1), "wo": ("up_done", 1, 1),
                     "qk1": ("plain_done", 2, 2), "v": ("v_done", 1, 1), "tq0": ("qlo_done", 2, 1),
                     "tk0": ("kT_done", 2, 1), "t4": ("h2T_done", 1, 1), "tq1": ("qlo_done", 2, 2),
                     "tk1": ("kT_done", 2, 2), "kv": ("state_done", 1, 1), "f1": ("lg_done", 1, 1)}

        x_dram = a["x"].rearrange("b (t p) c -> b p t c", p=P)
        out_dram = a["out"].rearrange("b (t p) c -> b p t c", p=P)

        block = ctx.enter_context(nc.Block())

        @block.sync
        def _(sp):
            sp.dma_start(cT[:], a["cT"].rearrange("(k p) b -> p k b", p=P)).then_inc(S["c_loaded"], 16)
            sp.dma_start(wmod, a["wmod"].rearrange("(k p) n -> p k n", p=P)).then_inc(S["wmod_loaded"], 16)

            def load(b):
                if b.first >= 2:
                    sp.wait_ge(S[f"x_loaded{b.parity}"], b.count(8, -8 * b.parity))
                sp.dma_start(X[:, b.at()], x_dram[b.at()].rearrange("o p t c -> p o t c")).then_inc(
                    S[f"x_loaded{b.parity}"], 16)

            load(Batch(0))
            load(Batch(1))
            sp.dma_start(wqkv[:], a["wqkv"].rearrange("(k p) n -> p k n", p=P)).then_inc(S["wqkv_loaded"], 16)
            with sp.Fori(0, NB // 2 - 1) as trip:
                for u in range(2):
                    load(Batch(2 + u, trip))

            def gates(b):
                if b.first >= 2:
                    sp.wait_ge(S["up2_done"], b.count(1, -1))
                src = gates_dram[b.at()].rearrange("o n -> (o n)").partition_broadcast(P)
                sp.dma_start(gate[b.parity][:], src.rearrange("p (g c) -> p g c", g=2)).then_inc(
                    S[f"gate_loaded{b.parity}"], 16)

            def store(b):
                sp.wait_ge(S["out_done"], b.count())
                sp.dma_start(out_dram[b.at()].rearrange("o p t c -> p o t c"), X[:, b.at()]).then_inc(
                    S["stored"], 16)

            sp.wait_ge(S["gates_stored"], 16)
            gates(Batch(0))
            gates(Batch(1))
            with sp.Fori(0, NB // 2 - 1) as trip:
                for u in range(2):
                    gates(Batch(2 + u, trip))
                    store(Batch(u, trip))
            store(Batch(NB - 2))
            store(Batch(NB - 1))
            sp.wait_ge(S["stored"], 16 * NB)

        @block.tensor
        def _(pe):
            def mm(out, lhsT, rhs, start=True, stop=True):
                return pe.matmul(out, lhsT, rhs, start=start, stop=stop)

            def free_bank(name, i):
                was = previous_use(name, i.first)
                if was:
                    who, off = was
                    s, per, extra = last_read[who]
                    pe.wait_ge(S[s], (i + off).count(per, extra))

            def mm3(out, lhs, rhs, start=True, stop=True):
                mm(out, lhs[0], rhs[0], start, False)
                mm(out, lhs[0], rhs[1], False, False)
                return mm(out, lhs[1], rhs[0], False, stop)

            pe.wait_ge(S["c_silu"], 1)
            pe.wait_ge(S["wmod_loaded"], 16)
            for m, part in enumerate((0, 1, 3, 4)):
                for n in range(NH):
                    for k in range(NH):
                        col = part * E + n * P
                        last = mm(ring_ps[:, 0, (m * NH + n) * NB:(m * NH + n + 1) * NB],
                                  wmod[:, k, col:col + P], csilu[:, k, :], k == 0, k == NH - 1)
            last.then_inc(S["mod_ps"], 1)
            for g in range(2):
                for k in range(NH):
                    last = mm(ring_ps[0:NB, 1, g * E:(g + 1) * E], csilu[:, k, :],
                              wmod[:, k, (2 + 3 * g) * E:(3 + 3 * g) * E], k == 0, k == NH - 1)
            last.then_inc(S["gate_ps"], 1)
            pe.wait_ge(S["mod_done"], 2)
            pe.wait_ge(S["gate_tmp"], 3)
            pe.wait_ge(S["consts_loaded"], 16 * 10)
            pe.wait_ge(S["w_lo"], 1)

            def t1(i):
                b = i + 2
                free_bank("t1", i)
                pe.wait_ge(S["xn_done"], b.count())
                for n in range(NH):
                    for t in range(NT):
                        c = (n * NT + t) * P
                        last = pe.transpose(bank("t1")[:, c:c + P], xn[b.parity][:, t, n * P:(n + 1) * P], ident[:])
                last.then_inc(S["t1_ps"], 1)

            def qk(i, t):
                b = i + 1
                free_bank(f"qk{t}", i)
                pe.wait_ge(S["hT_split"], b.count())
                for n in range(NH):
                    last = mm3(bank(f"qk{t}"), [x[:, n, t * P:(t + 1) * P] for x in hT_s[b.parity]],
                               [w[:, n, 0:2 * E] for w in wqkv_s], n == 0, n == NH - 1)
                last.then_inc(S["qk_ps"], 1)

            def values(i):
                b = i + 1
                free_bank("v", i)
                for t in range(NT):
                    for n in range(NH):
                        last = mm3(bank("v")[:, t * E:(t + 1) * E],
                                   [x[:, n, t * P:(t + 1) * P] for x in hT_s[b.parity]],
                                   [w[:, n, 2 * E:3 * E] for w in wqkv_s], n == 0, n == NH - 1)
                last.then_inc(S["v_ps"], 1)

            def t2(i, t):
                b = i + 1
                free_bank(f"tk{t}", i)
                pe.wait_ge(S["ks_done"], b.count(2, t + 1))
                for g in range(G):
                    src = ks[t][:, g * HG:(g + 1) * HG].rearrange("p h c d -> p (h c d)").bitcast(F32)
                    last = pe.transpose(bank(f"tk{t}")[:, g * P:(g + 1) * P], src, ident[:])
                last.then_inc(S["tk_ps"], 1)
                free_bank(f"tq{t}", i)
                pe.wait_ge(S["rotadd"], b.count(2, t + 1))
                pe.wait_ge(S["plain_done"], b.count(2, t + 1))
                for g in range(G):
                    src = qr[t][:, g * HG:(g + 1) * HG].rearrange("p h c d -> p (h c d)")
                    last = pe.transpose(bank(f"tq{t}")[:, g * P:(g + 1) * P], src, ident[:])
                last.then_inc(S["tq_ps"], 1)

            def v_heads(b, c, n):
                return v[b.parity][:, c, 4 * n:4 * n + 4].rearrange("p w (x d) -> p w x d", x=3)[:, :, 0:3:2, :]

            def kv(i):
                b = i + 1
                free_bank("kv", i)
                pe.wait_ge(S["kd_done"], b.count())
                pe.wait_ge(S["v_done"], b.count())
                for n in range(NH):
                    lhsT = kd[b.parity][:, 8 * n:8 * n + 8].rearrange("p h d -> p (h d)")
                    mm(bank("kv")[:, n * P:(n + 1) * P], lhsT, v_heads(b, 0, n))
                pe.wait_ge(S["qd_done"], b.count())
                for n in range(NH):
                    src = qd[b.parity][:, 8 * n:8 * n + 8].rearrange("p h d -> p (h d)")
                    last = pe.transpose(bank("kv")[:, E + n * P:E + (n + 1) * P], src, ident[:])
                last.then_inc(S["kv_ps"], 1)

            def scores(b, n):
                c, gp = n // 2, n % 2
                if b.first * 4 + n >= 2:
                    pe.wait_ge(S["pT_done"], b.count(4, n - 1))
                pe.wait_ge(S["kT_done"], b.count(2, c + 1))
                pe.wait_ge(S["qlo_done"], b.count(2, c + 1))
                for g2 in range(2):
                    for x in range(2):
                        for j in range(2):
                            rows = slice(64 * j, 64 * j + 64)
                            g = 2 * gp + g2
                            last = mm(sc_ps[:, 2 * gp + j, g2], kT[b.parity][rows, c, g, :],
                                      q_s[b.parity][x][rows, c, g], x == 0, x == 1)
                last.then_inc(S["sc_done"], 1)

            def inter(b):
                pe.wait_ge(S["state_done"], b.count())
                pe.wait_ge(S["qdT_done"], b.count())
                if b.first > 0:
                    pe.wait_ge(S["aT_done"], b.count(1, 0))
                for n in range(NH):
                    pe.matmul(o_ps[:, n, P:2 * P], state[b.parity][:, n, :], qdT[b.parity][:, n, :],
                              start=(n == 0), stop=False, skip_group_check=True)

            def pv(b, n):
                c, gp = n // 2, n % 2
                pe.wait_ge(S["pT_done"], b.count(4, n + 1))
                for ab in range(2):
                    for g2 in range(2):
                        for j in range(2):
                            strip = 2 * g2 + j
                            last = pe.matmul(o_ps[32 * strip:32 * strip + 32, gp, c * P:(c + 1) * P],
                                             v[b.parity][:, c, 4 * gp + strip, D * ab:D * ab + 2 * D],
                                             pT[gp][:, j, g2, ab, :], start=False, stop=(ab == 1),
                                             skip_group_check=True)
                last.then_inc(S["pv_done"], 1)

            def t5(i):
                b = i + -2
                free_bank("t5", i)
                pe.wait_ge(S["z_done"], b.count())
                for t in range(NT):
                    last = pe.transpose(bank("t5")[:, t * P:(t + 1) * P], z[b.parity][:, t, :], ident[:])
                last.then_inc(S["t5_ps"], 1)

            def sum_squares(i):
                b = i + -1
                free_bank("ss", i)
                pe.wait_ge(S["o_copied"], b.count(2, 1))
                for t in range(NT):
                    for n in range(NH):
                        last = mm(bank("ss")[:, t:t + 1], sqr[b.parity][:, n, t * P:(t + 1) * P], ones[:],
                                  n == 0, n == NH - 1)
                last.then_inc(S["ss_ps"], 1)

            def out_proj(i):
                b = i + -1
                free_bank("wo", i)
                pe.wait_ge(S["aT_done"], b.count())
                if b.first == 0:
                    pe.wait_ge(S["w_lo"], 4)
                for t in range(NT):
                    for n in range(NH):
                        last = mm3(bank("wo")[:, t * E:(t + 1) * E], [x[:, n, t * P:(t + 1) * P] for x in aT_s[b.parity]],
                                   [w[:, n, :] for w in wo_s], n == 0, n == NH - 1)
                last.then_inc(S["wo_ps"], 1)

            def t4(i):
                b = i + -1
                free_bank("t4", i)
                pe.wait_ge(S["xm_done"], b.count())
                for n in range(NH):
                    for t in range(NT):
                        c = (n * NT + t) * P
                        last = pe.transpose(bank("t4")[:, c:c + P], xm[b.parity][:, t, n * P:(n + 1) * P], ident[:])
                last.then_inc(S["t4_ps"], 1)

            def f1(i):
                b = i + -1
                free_bank("f1", i)
                pe.wait_ge(S["h2T_done"], b.count())
                if b.first == 0:
                    pe.wait_ge(S["w2_loaded"], 16 * 4)
                for t in range(NT):
                    for n in range(NH):
                        last = mm(bank("f1")[:, t * (NA + NE):(t + 1) * (NA + NE)], h2T[:, n, t * P:(t + 1) * P],
                                  war[:, n, :], n == 0, n == NH - 1)
                last.then_inc(S["f1_ps"], 1)

            def f2(i):
                b = i + -2
                free_bank("f2", i)
                pe.wait_ge(S["h2T_split"], b.count())
                pe.wait_ge(S["zlo_done"], b.count())
                for t in range(NT):
                    out = bank("f2")[:, t * E:(t + 1) * E]
                    for n in range(NH):
                        mm3(out, [x[:, n, t * P:(t + 1) * P] for x in h2T_s[b.parity]], [w[:, n, :] for w in wbase_s],
                            n == 0, False)
                    last = mm3(out, [x[:, t * P:(t + 1) * P] for x in zT_s[b.parity]], [w[:] for w in wb_s], False, True)
                last.then_inc(S["f2_ps"], 1)

            def iteration(i):
                front, mid, back, tail = i + 1, i, i + -1, i + -2
                if back.on:
                    pv(back, 3)
                if mid.on:
                    scores(mid, 0)
                if back.on:
                    sum_squares(i)
                if (i + 2).on:
                    t1(i)
                if mid.on:
                    scores(mid, 1)
                if back.on:
                    out_proj(i)
                if tail.on:
                    t5(i)
                if front.on:
                    qk(i, 0)
                if mid.on:
                    inter(mid)
                    pv(mid, 0)
                if front.on:
                    qk(i, 1)
                if tail.on:
                    f2(i)
                if front.on:
                    values(i)
                if back.on:
                    t4(i)
                if mid.on:
                    scores(mid, 2)
                if front.on:
                    t2(i, 0)
                if mid.on:
                    pv(mid, 1)
                    scores(mid, 3)
                if back.on:
                    f1(i)
                if mid.on:
                    pv(mid, 2)
                if front.on:
                    t2(i, 1)
                    kv(i)

            pipeline(pe, iteration, -2, NB + 1)

        @block.scalar
        def _(act):
            loads = (("qdecay", qdecay), ("kdecay", kdecay), ("rcos", rcos), ("rsin", rsin), ("ident", ident),
                     ("diag", diag), ("dmask", dmask), ("least", least),
                     ("even_odd", even_odd))
            for name, dst in loads:
                act.dma_start(dst[:], a[name]).then_inc(S["consts_loaded"], 16)
            act.dma_start(rmsw[:], a["rms_w"]).then_inc(S["consts_loaded"], 16)
            act.wait_ge(S["c_loaded"], 16)
            act.activation(ctmp[:, 0], cT[:], ACT.Exp, scale=-1.0).then_inc(S["c_exp"], 1)
            act.wait_ge(S["mod_done"], 2)

            def h_evac(b, src, full, hi, shift, scale, ready, split, done):
                act.wait_ge(S[ready], b.count())
                if b.first > 0:
                    act.wait_ge(S[split], b.count(1, 0))
                k = b.at()
                for dst in (full, hi):
                    for n in range(NH):
                        last = act.activation(dst[:, n, :], src[:, n * NT * P:(n + 1) * NT * P], ACT.Identity,
                                              bias=modT[:, shift, n, k], scale=modT[:, scale, n, k])
                last.then_inc(S[done], 1)

            def plain_dims(i, t):
                b = i + 1
                qkv = bank(f"qk{t}").rearrange("p (w h d) -> p w h d", w=2, d=D)
                act.wait_ge(S["rotmul"], b.count(2, t + 1))
                act.activation(kr[t][:, :, 8:16], qkv[:, 1, :, 8:16], ACT.Copy)
                act.activation(qr[t][:, :, :, 8:16], qkv[:, 0, :, 8:16].unsqueeze(2).broadcast_to([P, H, 2, 8]),
                               ACT.Copy).then_inc(S["plain_done"], 1)

            def k_high(i, t):
                b = i + 1
                act.wait_ge(S["rotadd"], b.count(2, t + 1))
                act.wait_ge(S["plain_done"], b.count(2, t + 1))
                act.activation(ks[t][:, :, 0, :], kr[t][:], ACT.Copy).then_inc(S["khi_done"], 1)

            def values_evac(b):
                act.wait_ge(S["v_ps"], b.count())
                for t in range(NT):
                    dst = v[b.parity][:, t].rearrange("p w (x d) -> p w x d", x=3)[:, :, 0:3:2, :]
                    last = act.activation(dst, bank("v")[:, t * E:(t + 1) * E].rearrange(
                        "p (w x d) -> p w x d", x=2, d=D), ACT.Copy)
                last.then_inc(S["v_done"], 1)

            def q_high(b, t):
                act.wait_ge(S["tq_ps"], b.count(2, t + 1))
                for ab in range(2):
                    last = act.activation(q_s[b.parity][0][:, t, :, ab, :],
                                          bank(f"tq{t}").rearrange("p (g c) -> p g c", g=G), ACT.Copy,
                                          scale=even_odd[:, ab:ab + 1])
                last.then_inc(S["qhi_done"], 1)

            def k_evac(b, t):
                act.wait_ge(S["tk_ps"], b.count(2, t + 1))
                act.activation(kT[b.parity][:, t], bank(f"tk{t}").rearrange("p (g c) -> p g c", g=G),
                               ACT.Copy).then_inc(S["kT_done"], 1)

            def iteration(i):
                front, back, tail, ahead_b = i + 1, i + -1, i + -2, i + 2
                if tail.on:
                    act.wait_ge(S["lsub_done"], tail.count())
                    act.activation(lexp[:, tail.parity], lsub[:, tail.parity], ACT.Exp).then_inc(S["lexp_done"], 1)
                if back.on:
                    act.wait_ge(S["pv_done"], back.count(4, 4))
                    act.activation(sqr[back.parity][:], o_ps[:], ACT.Square).then_inc(S["o_copied"], 1)
                    act.activation(aT_s[back.parity][0][:], o_ps[:], ACT.Copy).then_inc(S["o_copied"], 1)
                if ahead_b.on:
                    h_evac(ahead_b, bank("t1"), hT, hT_s[ahead_b.parity][0], SA, CA, "t1_ps", "hT_split", "hT_done")
                if tail.on:
                    act.wait_ge(S["t5_ps"], tail.count())
                    act.activation(zT_s[tail.parity][0][:], bank("t5")[:, 0:NT * P], ACT.Copy).then_inc(S["zhi_done"], 1)
                if front.on:
                    plain_dims(i, 0)
                    k_high(i, 0)
                    plain_dims(i, 1)
                    values_evac(front)
                if back.on:
                    h_evac(back, bank("t4"), h2T, h2T_s[back.parity][0], SB, CB, "t4_ps", "h2T_split", "h2T_done")
                if front.on:
                    k_high(i, 1)
                    q_high(front, 0)
                    k_evac(front, 0)
                if back.on:
                    act.wait_ge(S["f1_ps"], back.count())
                    if back.first >= 2:
                        act.wait_ge(S["z_done"], back.count(1, -1))
                    act.activation(f1s[:, back.parity], bank("f1")[:, 0:NT * (NA + NE)].rearrange(
                        "p (t c) -> p t c", t=NT), ACT.Copy).then_inc(S["lg_done"], 1)
                if front.on:
                    k_evac(front, 1)
                    q_high(front, 1)
                    act.wait_ge(S["kv_ps"], front.count())
                    act.activation(qdT[front.parity][:], bank("kv")[:, E:2 * E].rearrange("p (n c) -> p n c", n=NH),
                                   ACT.Copy).then_inc(S["qdT_done"], 1)

            pipeline(act, iteration, -2, NB + 1)

        @block.gpsimd
        def _(pool):
            pool.dma_start(wo_in[:], a["wo"].rearrange("(k p) n -> p k n", p=P)).then_inc(S["w2_loaded"], 16)
            pool.dma_start(war[:], a["war"].rearrange("(k p) n -> p k n", p=P)).then_inc(S["w2_loaded"], 16)
            pool.dma_start(wbase[:], a["wbase"].rearrange("(k p) n -> p k n", p=P)).then_inc(S["w2_loaded"], 16)
            pool.dma_start(wb[:], a["wb"]).then_inc(S["w2_loaded"], 16)
            for p in range(2):
                pool.memset(v[p][:], 0.0)
            pool.memset(ones[:], 1.0)
            pool.memset(half[:], -0.5).then_inc(S["const_done"], 1)
            pool.wait_ge(S["w2_loaded"], 16 * 4)
            pool.wait_ge(S["consts_loaded"], 16 * 10)
            for n in range(NH):
                last = pool.tensor_scalar(wo[:, n, :], wo_in[:, n, :], rmsw[:, n:n + 1], None, ALU.mult)
            last.then_inc(S["wo_scaled"], 1)
            pool.wait_ge(S["const_done"], 1)
            pool.wait_ge(S["gates_done"], 1)
            pool.dma_start(gates_dram, gates16[:]).then_inc(S["gates_stored"], 16)

            def rsqrt(b, var, mul, tmp, out, ready, mid_sem, done):
                hold(pool, S[ready], b.count(), S["pool_held"])
                pool.tensor_scalar(tmp, var, mul, EPS, ALU.mult, ALU.add).then_inc(S[mid_sem], 1)
                pool.wait_ge(S[mid_sem], b.count())
                pool.tensor_tensor(out, tmp, half[:], ALU.pow).then_inc(S[done], 1)

            def rotate(i, t):
                b = i + 1
                pool.wait_ge(S["rotmul"], b.count(2, t + 1))
                pool.tensor_tensor(kr[t][:, :, 0:8], rotc[t][:, H:2 * H, :], rots[t][:, H:2 * H, :], ALU.add)
                pool.tensor_tensor(qr[t][:, :, :, 0:8], rotc[t][:, 0:H, :].unsqueeze(2).broadcast_to([P, H, 2, 8]),
                                   rots[t][:, 0:H, :].unsqueeze(2).broadcast_to([P, H, 2, 8]),
                                   ALU.add).then_inc(S["rotadd"], 1)

            def k_low(i, t):
                b = i + 1
                pool.wait_ge(S["rotadd"], b.count(2, t + 1))
                pool.wait_ge(S["khi_done"], b.count(2, t + 1))
                pool.tensor_tensor(ks[t][:, :, 1, :], kr[t][:], ks[t][:, :, 0, :].bitcast(F32),
                                   ALU.subtract).then_inc(S["ks_done"], 1)
                if t == 0:
                    pool.tensor_tensor(kd[b.parity][:], kr[0][:], kdecay[:].unsqueeze(2).broadcast_to([P, H, D]),
                                       ALU.mult).then_inc(S["kd_done"], 1)
                else:
                    pool.tensor_tensor(qd[b.parity][:], qr[1][:, :, 0, :], qdecay[:].unsqueeze(2).broadcast_to([P, H, D]),
                                       ALU.mult).then_inc(S["qd_done"], 1)

            def h_low(b, full, split, ready, done):
                pool.wait_ge(S[ready], b.count())
                pool.tensor_tensor(split[1][:], full[:], split[0][:].bitcast(F32), ALU.subtract).then_inc(S[done], 1)

            def iteration(i):
                front, back, tail, ahead_b, stats_b = i + 1, i + -1, i + -2, i + 2, i + 3
                p = back.parity
                if back.on:
                    pool.wait_ge(S["ms_done"], back.count())
                    pool.tensor_tensor(rrms[:, p], ms[:, p], half[:], ALU.pow).then_inc(S["rrms_done"], 1)
                    hold(pool, S["up_done"], back.count(), S["pool_held"])
                    pool.tensor_tensor(X[:, back.at()], X[:, back.at()], up[back.parity].unsqueeze(1),
                                       ALU.add).then_inc(S["x1_done"], 1)
                if front.on:
                    rotate(i, 0)
                if back.on:
                    rsqrt(back, mv2[:, p, :, 1], 1.0, ve2[:, p], rstd2[:, p], "mean2", "ve2_done", "rstd2_done")
                if front.on:
                    k_low(i, 0)
                    rotate(i, 1)
                if stats_b.on:
                    q = stats_b.parity
                    rsqrt(stats_b, mv1[:, q, :, 1], 1.0, ve1[:, q], rstd1[:, q], "mean1", "ve1_done", "rstd1_done")
                if tail.on:
                    hold(pool, S["up2_done"], tail.count(), S["pool_held"])
                    pool.tensor_tensor(X[:, tail.at()], X[:, tail.at()], up2[tail.parity][:].unsqueeze(1),
                                       ALU.add).then_inc(S["out_done"], 1)
                if front.on:
                    k_low(i, 1)
                if back.on:
                    pool.wait_ge(S["lg_done"], back.count())
                    if back.first > 0:
                        pool.wait_ge(S["ahead_done"], back.count(1, 0))
                    pool.tensor_tensor(ldiff[:], lg[:, p].unsqueeze(2).broadcast_to([P, NT, NE, NE]),
                                       lg[:, p].unsqueeze(3).broadcast_to([P, NT, NE, NE]),
                                       ALU.subtract).then_inc(S["ldiff_done"], 1)
                    h_low(back, h2T, h2T_s[p], "h2T_done", "h2T_split")
                if ahead_b.on:
                    h_low(ahead_b, hT, hT_s[ahead_b.parity], "hT_done", "hT_split")

            pipeline(pool, iteration, -3, NB + 1)

        @block.vector
        def _(dve):
            dve.wait_ge(S["c_exp"], 1)
            dve.tensor_scalar(ctmp[:, 1], ctmp[:, 0], 1.0, None, ALU.add).then_inc(S["c_tmp"], 1)
            dve.wait_ge(S["c_tmp"], 1)
            dve.reciprocal(ctmp[:, 2], ctmp[:, 1]).then_inc(S["c_tmp"], 1)
            dve.wait_ge(S["c_tmp"], 2)
            dve.tensor_tensor(csilu[:], cT[:], ctmp[:, 2], ALU.mult).then_inc(S["c_silu"], 1)
            dve.wait_ge(S["mod_ps"], 1)
            mods = ring_ps[:, 0, 0:4 * NH * NB].rearrange("p (m n b) -> p m n b", m=4, n=NH)
            for first, plus in ((SA, 0.0), (CA, 1.0)):
                ins = dve.tensor_scalar(modT[:, first::2], mods[:, first::2], plus, None, ALU.add)
                ins.then_inc(S["mod_done"], 1)
            dve.wait_ge(S["gate_ps"], 1)
            gps = ring_ps[0:NB, 1, :]
            dve.tensor_scalar(gstep[:], gps, 0.0, 2.0, ALU.is_ge, ALU.mult).then_inc(S["gate_tmp"], 1)
            dve.wait_ge(S["gate_tmp"], 1)
            dve.tensor_scalar(gsign[:], gstep[:], -1.0, None, ALU.add).then_inc(S["gate_tmp"], 1)
            dve.wait_ge(S["gate_tmp"], 2)
            dve.tensor_tensor(gmag[:], gps, gsign[:], ALU.mult).then_inc(S["gate_tmp"], 1)
            dve.wait_ge(S["gate_tmp"], 3)
            dve.scalar_tensor_tensor(out=gates16[:], in0=gmag[:], scalar=0.25, in1=gsign[:], op0=ALU.max,
                                     op1=ALU.mult).then_inc(S["gates_done"], 1)

            def stats(x, st, b, stats_sem):
                for t in range(NT):
                    last = dve.bn_stats(st[:, b.parity, t, :], x[:, t, :])
                last.then_inc(S[stats_sem], 1)

            def mean(st, mv, b, stats_sem, mean_sem):
                hold(dve, S[stats_sem], b.count(), S["dve_held"])
                for t in range(NT):
                    last = dve.bn_aggr(mv[:, b.parity, t, :], st[:, b.parity, t, :])
                last.then_inc(S[mean_sem], 1)

            def normalise(x, dst, mv, rstd, b):
                for t in range(NT):
                    last = dve.tensor_scalar(dst[:, t, :], x[:, t, :], mv[:, b.parity, t, 0:1],
                                             rstd[:, b.parity, t:t + 1], ALU.subtract, ALU.mult)
                return last

            def x_of(b):
                return X[:, b.at()].rearrange("p o t c -> p (o t) c")

            def mask(b, n):
                c, r = n // 2, n % 2
                dve.wait_ge(S["sc_done"], b.count(4, n + 1))
                if b.first * 4 + n >= 2:
                    dve.wait_ge(S["pv_done"], b.count(4, n - 1))
                flat = "p j g x t -> p (j g x t)"
                dve.tensor_tensor(pT[r][:].rearrange(flat), sc_ps[:, 2 * r:2 * r + 2].rearrange(flat),
                                  dmask[:, r].rearrange(flat), ALU.mult).then_inc(S["pT_done"], 1)

            def rot(i, t):
                b = i + 1
                dve.wait_ge(S["qk_ps"], b.count(2, t + 1))
                if b.first > 0:
                    dve.wait_ge(S["rotadd"], b.count(2, t - 1))
                qkv = bank(f"qk{t}").rearrange("p (h d) -> p h d", d=D)
                dve.tensor_tensor(rotc[t][:], qkv[:, :, 0:8], rcos[:, t].unsqueeze(1).broadcast_to([P, 2 * H, 8]),
                                  ALU.mult)
                dve.tensor_tensor(rots[t][:, :, 0:4], qkv[:, :, 4:8],
                                  rsin[:, t, 0:4].unsqueeze(1).broadcast_to([P, 2 * H, 4]), ALU.mult)
                dve.tensor_tensor(rots[t][:, :, 4:8], qkv[:, :, 0:4],
                                  rsin[:, t, 4:8].unsqueeze(1).broadcast_to([P, 2 * H, 4]),
                                  ALU.mult).then_inc(S["rotmul"], 1)

            def q_low(i, t):
                b = i + 1
                p = b.parity
                dve.wait_ge(S["qhi_done"], b.count(2, t + 1))
                for ab in range(2):
                    last = dve.scalar_tensor_tensor(
                        out=q_s[p][1][:, t, :, ab, :], in0=bank(f"tq{t}").rearrange("p (g c) -> p g c", g=G),
                        scalar=even_odd[:, ab:ab + 1], in1=q_s[p][0][:, t, :, ab, :].bitcast(F32), op0=ALU.mult,
                        op1=ALU.subtract)
                last.then_inc(S["qlo_done"], 1)

            def ln1_stats(i):
                b = i + 3
                dve.wait_ge(S[f"x_loaded{b.parity}"], b.count(8, 16 - 8 * b.parity))
                stats(x_of(b), stat1, b, "stats1")

            def ln1_apply(i):
                b = i + 3
                dve.wait_ge(S["rstd1_done"], b.count())
                if b.first >= 2:
                    dve.wait_ge(S["t1_ps"], b.count(1, -1))
                normalise(x_of(b), xn[b.parity], mv1, rstd1, b).then_inc(S["xn_done"], 1)

            dve.wait_ge(S["consts_loaded"], 16 * 10)

            def split_weights(n, src, dst):
                dve.tensor_copy(dst[0], src).then_inc(S["w_hi"], 1)
                dve.wait_ge(S["w_hi"], n)
                dve.tensor_tensor(dst[1], src, dst[0].bitcast(F32), ALU.subtract).then_inc(S["w_lo"], 1)

            dve.wait_ge(S["wqkv_loaded"], 16)
            split_weights(1, wqkv[:], [w[:] for w in wqkv_s])

            def z_low(b):
                dve.wait_ge(S["zhi_done"], b.count())
                dve.tensor_tensor(zT_s[b.parity][1][:], bank("t5")[:, 0:NT * P], zT_s[b.parity][0][:].bitcast(F32),
                                  ALU.subtract).then_inc(S["zlo_done"], 1)

            def a_low(b):
                dve.wait_ge(S["o_copied"], b.count(2, 2))
                dve.tensor_tensor(aT_s[b.parity][1][:], o_ps[:], aT_s[b.parity][0][:].bitcast(F32),
                                  ALU.subtract).then_inc(S["aT_done"], 1)

            def mean_square(b):
                dve.wait_ge(S["ss_ps"], b.count())
                dve.tensor_scalar(ms[:, b.parity], bank("ss")[:, 0:NT], 1.0 / E, EPS, ALU.mult, ALU.add).then_inc(
                    S["ms_done"], 1)

            def gate_attention(b):
                p = b.parity
                dve.wait_ge(S[f"gate_loaded{p}"], b.count(8, 16 - 8 * p))
                dve.wait_ge(S["wo_ps"], b.count())
                dve.wait_ge(S["rrms_done"], b.count())
                for t in range(NT):
                    last = dve.scalar_tensor_tensor(
                        out=up[p][:, t, :], in0=bank("wo")[:, t * E:(t + 1) * E], scalar=rrms[:, p, t:t + 1],
                        in1=gate[p][:, 0, :], op0=ALU.mult, op1=ALU.mult)
                last.then_inc(S["up_done"], 1)

            def gate_experts(b):
                dve.wait_ge(S["f2_ps"], b.count())
                gb = gate[b.parity][:, 1, :].unsqueeze(1).broadcast_to([P, NT, E])
                dve.tensor_tensor(up2[b.parity][:], bank("f2").rearrange("p (t c) -> p t c", t=NT), gb,
                                  ALU.mult).then_inc(S["up2_done"], 1)

            def take_state(b):
                dve.wait_ge(S["kv_ps"], b.count())
                dve.wait_ge(S["qdT_done"], b.count())
                dve.tensor_tensor(state[b.parity][:], bank("kv")[:, 0:E].rearrange("p (n c) -> p n c", n=NH),
                                  diag[:].unsqueeze(1).broadcast_to([P, NH, P]),
                                  ALU.mult).then_inc(S["state_done"], 1)

            def logits_less_max(b):
                p = b.parity
                dve.wait_ge(S["lg_done"], b.count())
                dve.reduce_max(lmax[:, p], lg[:, p], AX_X).then_inc(S["lmax_done"], 1)
                dve.wait_ge(S["lmax_done"], b.count())
                dve.tensor_tensor(lsub[:, p], lg[:, p], lmax[:, p].unsqueeze(2).broadcast_to([P, NT, NE]),
                                  ALU.subtract).then_inc(S["lsub_done"], 1)

            def expert_ranks(b):
                p = b.parity
                dve.wait_ge(S["ldiff_done"], b.count())
                dve.tensor_tensor(ahead[:], ldiff[:], least[:].unsqueeze(1).broadcast_to([P, NT, NE, NE]),
                                  ALU.is_ge).then_inc(S["ahead_done"], 1)
                dve.wait_ge(S["ahead_done"], b.count())
                dve.reduce_sum(rank[:, p], ahead[:], AX_X).then_inc(S["rank_done"], 1)

            def route(b):
                p = b.parity
                dve.wait_ge(S["rank_done"], b.count())
                dve.wait_ge(S["lexp_done"], b.count())
                dve.scalar_tensor_tensor(out=wsel[:, p], in0=rank[:, p], scalar=2.0, in1=lexp[:, p],
                                         op0=ALU.is_lt, op1=ALU.mult).then_inc(S["wsel_done"], 1)
                dve.wait_ge(S["wsel_done"], b.count())
                dve.reduce_sum(wsum[:, p], wsel[:, p], AX_X).then_inc(S["wsum_done"], 1)
                dve.wait_ge(S["wsum_done"], b.count())
                dve.reciprocal(wrec[:, p], wsum[:, p]).then_inc(S["wrec_done"], 1)
                dve.wait_ge(S["wrec_done"], b.count())
                dve.scalar_tensor_tensor(out=wexp[:, p], in0=wsel[:, p], scalar=SCALING,
                                         in1=wrec[:, p].unsqueeze(2).broadcast_to([P, NT, NE]),
                                         op0=ALU.mult, op1=ALU.mult).then_inc(S["wexp_done"], 1)
                dve.wait_ge(S["wexp_done"], b.count())
                dve.tensor_tensor(z[p][:].rearrange("p t (e r) -> p t e r", r=R),
                                  f1s[:, p, :, 0:NA].rearrange("p t (e r) -> p t e r", r=R),
                                  wexp[:, p].unsqueeze(3).broadcast_to([P, NT, NE, R]),
                                  ALU.mult).then_inc(S["z_done"], 1)

            def iteration(i):
                front, mid, back, tail = i + 1, i, i + -1, i + -2
                pb = back.parity
                if back.first == 0:
                    dve.wait_ge(S["wo_scaled"], 1)
                    split_weights(2, wo[:], [w[:] for w in wo_s])
                    split_weights(3, wbase[:], [w[:] for w in wbase_s])
                    split_weights(4, wb[:], [w[:] for w in wb_s])
                if back.on:
                    a_low(back)
                    mean_square(back)
                if mid.on:
                    mask(mid, 0)
                if tail.on:
                    route(tail)
                if back.on:
                    gate_attention(back)
                if mid.on:
                    mask(mid, 1)
                if front.on:
                    rot(i, 0)
                if tail.on:
                    z_low(tail)
                if back.on:
                    dve.wait_ge(S["x1_done"], back.count())
                    stats(x_of(back), stat2, back, "stats2")
                    mean(stat2, mv2, back, "stats2", "mean2")
                if front.on:
                    rot(i, 1)
                if back.on:
                    dve.wait_ge(S["rstd2_done"], back.count())
                    normalise(x_of(back), xm[pb], mv2, rstd2, back).then_inc(S["xm_done"], 1)
                if tail.on:
                    gate_experts(tail)
                if (i + 3).on:
                    ln1_stats(i)
                    mean(stat1, mv1, i + 3, "stats1", "mean1")
                if mid.on:
                    mask(mid, 2)
                if (i + 3).on:
                    ln1_apply(i)
                if front.on:
                    q_low(i, 0)
                if mid.on:
                    mask(mid, 3)
                if back.on:
                    logits_less_max(back)
                    expert_ranks(back)
                if front.on:
                    q_low(i, 1)
                    take_state(front)

            pipeline(dve, iteration, -3, NB + 1)


def shape_tables():
    import math

    import numpy as np

    f = np.float32
    start = 2.0 ** (-2.0 ** (-(math.log2(H) - 3)))
    slopes = np.array([start * start ** i for i in range(H)], dtype=f)
    r = np.exp(-slopes.astype(np.float64)).astype(f).astype(np.float64)
    i = np.arange(P, dtype=np.float64)
    diff = i[None, :] - i[:, None]
    decay = np.where(diff[None] >= 0, r[:, None, None] ** np.maximum(diff, 0)[None], 0.0)
    dmask = decay.reshape(2, 2, 2, 2, P, P).transpose(4, 0, 2, 1, 3, 5)
    freq = np.concatenate([(f(1.0 / 1024.0) ** np.linspace(0.0, 1.0, D // 4, dtype=f)).astype(f)])
    theta = (np.arange(NT * P, dtype=f)[:, None] * freq[None, :]).astype(f).astype(np.float64)
    cos, sin = np.cos(theta), np.sin(theta)
    rcos = np.concatenate([cos, cos], axis=1).reshape(NT, P, 8).transpose(1, 0, 2)
    rsin = np.concatenate([sin, -sin], axis=1).reshape(NT, P, 8).transpose(1, 0, 2)
    row = np.arange(P)
    diag = row[:, None] // D == row[None, :] // D
    even_odd = np.stack([row // 32 % 2 == 0, row // 32 % 2 == 1], axis=1)
    e = np.arange(NE)
    ej = e[None, :] - e[:, None]
    least = np.broadcast_to(np.where(ej < 0, 0.0, np.where(ej > 0, np.finfo(f).tiny, np.finfo(f).max)), (P, NE, NE))
    return {k: np.ascontiguousarray(t, dtype=f) for k, t in {
        "dmask": dmask, "qdecay": (r[:, None] ** (i[None] + 1.0)).T, "kdecay": (r[:, None] ** (P - 1.0 - i[None])).T,
        "rcos": rcos, "rsin": rsin, "ident": np.eye(P), "diag": diag, "even_odd": even_odd, "least": least}.items()}


def kernel(**inputs):
    import numpy as np
    import concourse.bacc as bacc
    from concourse.bass_utils import run_bass_kernel_spmd as run

    f = {k[3:]: np.asarray(t) for k, t in inputs.items()}
    order = np.concatenate([np.r_[0:4, 8:12, 4:8, 12:16] + D * h for h in range(H)])
    arrays = {
        "x": f["attn_x"], "cT": f["c"].T, "wmod": f["wmod"],
        "wqkv": np.concatenate([f["attn_Wq"][:, order], f["attn_Wk"][:, order], f["attn_Wv"]], axis=1),
        "wo": f["attn_Wo"], "rms_w": f["attn_rms_w"].reshape(NH, P).T,
        "war": np.concatenate([f["ffn_lora_A"].reshape(NA, E).T, f["ffn_router_w"].T], axis=1),
        "wbase": f["ffn_weight"].T, "wb": f["ffn_lora_B"].transpose(0, 2, 1).reshape(NA, E),
    }
    arrays.update(shape_tables())
    arrays = {f"in_{k}": np.ascontiguousarray(t) for k, t in arrays.items()}
    nc = bacc.Bacc("TRN2", target_bir_lowering=False, num_devices=1)
    a = {k[3:]: nc.dram_tensor(k, t.shape, mybir.dt.from_np(t.dtype), kind="ExternalInput").ap()
         for k, t in arrays.items()}
    a["out"] = nc.dram_tensor("out_0", (NB, NT * P, E), F32, kind="ExternalOutput").ap()
    build(nc, a)
    r = run(nc, [arrays], core_ids=[0])
    return r.results[0]["out_0"]
```

```python
from contextlib import ExitStack

import concourse.bass as bass
from concourse import mybir

F32 = mybir.dt.float32
F32R = mybir.dt.float32r
ALU = mybir.AluOpType
ACT = mybir.ActivationFunctionType
AX_X = mybir.AxisListType.X

P = 128
NB = 16
NT = 2
E = 256
NH = E // P
H = 16
D = E // H
G = 4
HG = H // G
NE = 8
R = 16
NA = NE * R
EPS = 1e-5
SCALING = 2.0
SA, CA, SB, CB = range(4)


class Batch:

    def __init__(self, first, trip=None):
        self.first, self.trip = first, trip

    def __add__(self, k):
        return Batch(self.first + k, self.trip)

    @property
    def on(self):
        return 0 <= self.first < NB

    @property
    def parity(self):
        return self.first % 2

    def count(self, per=1, extra=1):
        at = per * self.first + extra
        return at if self.trip is None else self.trip * (2 * per) + at

    def at(self):
        return bass.ds(self.count(1, 0), 1)


LOOP_FIRST, LOOP_TRIPS = 3, 5


def pipeline(eng, iteration, first, last):
    for i in range(first, LOOP_FIRST):
        iteration(Batch(i))
    with eng.Fori(0, LOOP_TRIPS) as trip:
        for u in range(2):
            iteration(Batch(LOOP_FIRST + u, trip))
    for i in range(LOOP_FIRST + 2 * LOOP_TRIPS, last + 1):
        iteration(Batch(i))


def hold(eng, semaphore, value, held):
    eng.wait_ge(semaphore, value)
    eng.sem_inc(held, 1)


RING = [("t1", 2), ("ss", -1), ("wo", -1), ("t5", -2), ("qk0", 1), ("qk1", 1), ("f2", -2), ("v", 1), ("t4", -1),
        ("tk0", 1), ("tq0", 1), ("f1", -1), ("tk1", 1), ("tq1", 1), ("kv", 1)]
NRING = 3
SLOT = {name: n % NRING for n, (name, _) in enumerate(RING)}


def previous_use(name, i):
    n = [r[0] for r in RING].index(name)
    back = 0
    while True:
        n -= NRING
        if n < 0:
            n += len(RING)
            back += 1
        who, off = RING[n]
        b = i - back + off
        if i - back < -2:
            return None
        if 0 <= b < NB:
            return who, off - back


def build(nc, a):
    ctx = ExitStack()
    with ctx:
        def sb(name, shape, dt=F32):
            return ctx.enter_context(nc.sbuf_tensor(name, shape, dt))

        def ps(name, shape):
            return ctx.enter_context(nc.psum_tensor(name, shape, F32))

        def sem(name):
            return ctx.enter_context(nc.semaphore(name))

        X = sb("X", [P, NB, NT, E])
        scratch = sb("scratch", [P, NH * 6 * E])
        wmod = scratch[:].rearrange("p (k n) -> p k n", k=NH)
        xm, up = ([scratch[:, (2 * w + p) * NT * E:(2 * w + p + 1) * NT * E].rearrange("p (t c) -> p t c", t=NT)
                   for p in range(2)] for w in (1, 2))
        pT = [scratch[:, 0:8 * P].rearrange("p (j g x t) -> p j g x t", j=2, g=2, x=2),
              sb("pT1", [P, 2, 2, 2, P])]
        cT = sb("cT", [P, NH, NB])
        ctmp = sb("ctmp", [P, 3, NH, NB])
        csilu = sb("csilu", [P, NH, NB])
        modT = sb("modT", [P, 4, NH, NB])
        gstep, gsign, gmag, gates16 = (scratch[0:NB, (2 + n) * NT * E:(3 + n) * NT * E] for n in range(4))
        scratch2 = sb("scratch2", [P, 5 * NT * E])
        wqkv = scratch2[:, 0:6 * E].rearrange("p (k n) -> p k n", k=NH)
        wo_in = scratch2[:, 6 * E:8 * E].rearrange("p (k n) -> p k n", k=NH)
        wbase = scratch2[:, 8 * E:10 * E].rearrange("p (k n) -> p k n", k=NH)
        sqr = [scratch2[:, 2 * p * E:2 * (p + 1) * E].rearrange("p (n t) -> p n t", n=NH) for p in range(2)]
        up2 = [scratch2[:, (4 + 2 * p) * E:(6 + 2 * p) * E].rearrange("p (t c) -> p t c", t=NT) for p in range(2)]
        z = [scratch2[:, (8 + p) * E:(9 + p) * E].rearrange("p (t c) -> p t c", t=NT) for p in range(2)]
        rmsw = sb("rmsw", [P, NH])
        wo = sb("wo", [P, NH, E])
        wqkv_s = [sb(f"wqkv_{x}", [P, NH, 3 * E], F32R) for x in ("hi", "lo")]
        wo_s = [sb(f"wo_{x}", [P, NH, E], F32R) for x in ("hi", "lo")]
        wbase_s = [sb(f"wbase_{x}", [P, NH, E], F32R) for x in ("hi", "lo")]
        wb_s = [sb(f"wb_{x}", [P, E], F32R) for x in ("hi", "lo")]
        war = sb("war", [P, NH, NA + NE])
        wb = sb("wb", [P, E])
        dmask = sb("dmask", [P, 2, 2, 2, 2, P])
        qdecay = sb("qdecay", [P, H])
        kdecay = sb("kdecay", [P, H])
        rcos = sb("rcos", [P, NT, 8])
        rsin = sb("rsin", [P, NT, 8])
        ident = sb("ident", [P, P])
        diag = sb("diag", [P, P])
        even_odd = sb("even_odd", [P, 2])
        ones = sb("ones", [P, 1])
        least = sb("least", [P, NE, NE])
        minus_half = sb("minus_half", [P, NT])

        stat1 = sb("stat1", [P, 2, NT, 6])
        mv1 = sb("mv1", [P, 2, NT, 2])
        ve1 = sb("ve1", [P, 2, NT])
        rstd1 = sb("rstd1", [P, 2, NT])
        gate = [sb(f"gate{p}", [P, 2, E]) for p in range(2)]
        xn = [sb(f"xn{p}", [P, NT, E]) for p in range(2)]
        hT = sb("hT", [P, NH, NT * P])
        hT_s = [[sb(f"hT{x}{p}", [P, NH, NT * P], F32R) for x in ("hi", "lo")] for p in range(2)]
        rotc = [sb(f"rotc{t}", [P, 2 * H, 8]) for t in range(NT)]
        rots = [sb(f"rots{t}", [P, 2 * H, 8]) for t in range(NT)]
        qr = [sb(f"qr{t}", [P, H, 2, D]) for t in range(NT)]
        kr = [sb(f"kr{t}", [P, H, D]) for t in range(NT)]
        ks = [sb(f"ks{t}", [P, H, 2, D], F32R) for t in range(NT)]
        kd = [sb(f"kd{p}", [P, H, D]) for p in range(2)]
        qd = [sb(f"qd{p}", [P, H, D]) for p in range(2)]
        qdT = [sb(f"qdT{p}", [P, NH, P]) for p in range(2)]
        v = [sb(f"v{p}", [P, NT, H // 2, 3 * D]) for p in range(2)]
        q_s = [[sb(f"q{x}{p}", [P, NT, G, 2, P], F32R) for x in ("hi", "lo")] for p in range(2)]
        kT = [sb(f"kT{p}", [P, NT, G, P], F32R) for p in range(2)]
        state = [sb(f"state{p}", [P, NH, P]) for p in range(2)]
        ms = sb("ms", [P, 2, NT])
        rrms = sb("rrms", [P, 2, NT])
        aT_s = [[sb(f"aT{x}{p}", [P, NH, NT * P], F32R) for x in ("hi", "lo")] for p in range(2)]
        stat2 = sb("stat2", [P, 2, NT, 6])
        mv2 = sb("mv2", [P, 2, NT, 2])
        ve2 = sb("ve2", [P, 2, NT])
        rstd2 = sb("rstd2", [P, 2, NT])
        h2T = sb("h2T", [P, NH, NT * P])
        h2T_s = [[sb(f"h2T{x}{p}", [P, NH, NT * P], F32R) for x in ("hi", "lo")] for p in range(2)]
        f1s = sb("f1s", [P, 2, NT, NA + NE])
        lg = f1s[:, :, :, NA:NA + NE]
        lmax = sb("lmax", [P, 2, NT])
        lsub = sb("lsub", [P, 2, NT, NE])
        lexp = sb("lexp", [P, 2, NT, NE])
        ldiff = sb("ldiff", [P, NT, NE, NE])
        ahead = sb("ahead", [P, NT, NE, NE])
        rank = sb("rank", [P, 2, NT, NE])
        wsel = sb("wsel", [P, 2, NT, NE])
        wsum = sb("wsum", [P, 2, NT])
        wrec = sb("wrec", [P, 2, NT])
        wexp = sb("wexp", [P, 2, NT, NE])
        zT_s = [[sb(f"zT{x}{p}", [P, NT * P], F32R) for x in ("hi", "lo")] for p in range(2)]

        sc_ps = ps("sc_ps", [P, 4, 2, 2, P])
        o_ps = ps("o_ps", [P, NH, NT * P])
        ring_ps = ps("ring_ps", [P, NRING, 512])

        def mod_ps(which):
            flat = sc_ps[:, which].rearrange("p g x t -> p (g x t)")
            return flat[:, 0:2 * NH * NB].rearrange("p (m n b) -> p m n b", m=2, n=NH)

        gate_ps = sc_ps[0:NB, 2].rearrange("p g x t -> p (g x t)")

        def bank(name):
            return ring_ps[:, SLOT[name], :]

        def f2_ps(b):
            return o_ps[:].rearrange("p n t -> p (n t)") if b.first == NB - 1 else bank("f2")

        gates_dram = nc.dram_tensor("gates_dram", [NB, 2 * E], F32, kind="Internal").ap()

        S = {n: sem(n) for n in (
            "c_loaded wmod1_loaded wmod2_loaded ident_loaded consts_loaded dmask_loaded wqkv_loaded w2_loaded "
            "gates_stored gate_loaded0 gate_loaded1 x_loaded0 x_loaded1 stored "
            "c_exp c_tmp c_silu mod1_ps mod2_ps gate_ps mod1_done mod2_done gate_tmp gates_done const_done "
            "wo_scaled w_hi w_lo "
            "stats1 mean1 ve1_done rstd1_done xn_done t1_ps hT_done hT_split qk_ps rotmul rotadd plain_done khi_done "
            "ks_done kd_done qd_done v_ps v_done tq_ps tk_ps qhi_done qlo_done kT_done kv_ps qdT_done state_done "
            "sc_done pT_done pv_done o_copied aT_done sqr_done ss_ps ms_done rrms_done wo_ps up_done x1_done stats2 mean2 "
            "ve2_done rstd2_done xm_done t4_ps h2T_done h2T_split f1_ps lg_done lmax_done lsub_done lexp_done "
            "ldiff_done ahead_done rank_done wsel_done wsum_done wrec_done wexp_done z_done t5_ps zhi_done zlo_done "
            "f2_ps up2_done out_done dve_held pool_held").split()}

        last_read = {"t5": ("zlo_done", 1, 1), "t1": ("hT_done", 1, 1), "f2": ("up2_done", 1, 1),
                     "ss": ("ms_done", 1, 1), "qk0": ("plain_done", 2, 1), "wo": ("up_done", 1, 1),
                     "qk1": ("plain_done", 2, 2), "v": ("v_done", 1, 1), "tq0": ("qlo_done", 2, 1),
                     "tk0": ("kT_done", 2, 1), "t4": ("h2T_done", 1, 1), "tq1": ("qlo_done", 2, 2),
                     "tk1": ("kT_done", 2, 2), "kv": ("state_done", 1, 1), "f1": ("lg_done", 1, 1)}

        x_dram = a["x"].rearrange("b (t p) c -> b p t c", p=P)
        out_dram = a["out"].rearrange("b (t p) c -> b p t c", p=P)

        block = ctx.enter_context(nc.Block())

        @block.sync
        def _(sp):
            sp.dma_start(cT[:], a["cT"].rearrange("(k p) b -> p k b", p=P)).then_inc(S["c_loaded"], 16)

            def load(b):
                if b.first >= 2:
                    sp.wait_ge(S[f"x_loaded{b.parity}"], b.count(8, -8 * b.parity))
                sp.dma_start(X[:, b.at()], x_dram[b.at()].rearrange("o p t c -> p o t c")).then_inc(
                    S[f"x_loaded{b.parity}"], 16)

            wmod_dram = a["wmod"].rearrange("(k p) n -> p k n", p=P)
            load(Batch(0))
            sp.dma_start(wmod[:, :, 0:2 * E], wmod_dram[:, :, 0:2 * E]).then_inc(S["wmod1_loaded"], 16)
            load(Batch(1))
            sp.dma_start(wqkv[:], a["wqkv"].rearrange("(k p) n -> p k n", p=P)).then_inc(S["wqkv_loaded"], 16)
            sp.dma_start(wmod[:, :, 2 * E:], wmod_dram[:, :, 2 * E:]).then_inc(S["wmod2_loaded"], 16)
            sp.dma_start(wo_in[:], a["wo"].rearrange("(k p) n -> p k n", p=P)).then_inc(S["w2_loaded"], 16)
            sp.dma_start(war[:], a["war"].rearrange("(k p) n -> p k n", p=P)).then_inc(S["w2_loaded"], 16)
            sp.dma_start(wbase[:], a["wbase"].rearrange("(k p) n -> p k n", p=P)).then_inc(S["w2_loaded"], 16)
            sp.dma_start(wb[:], a["wb"]).then_inc(S["w2_loaded"], 16)
            sp.dma_start(dmask[:], a["dmask"]).then_inc(S["dmask_loaded"], 16)
            with sp.Fori(0, NB // 2 - 1) as trip:
                for u in range(2):
                    load(Batch(2 + u, trip))

            def gates(b):
                if b.first >= 2:
                    sp.wait_ge(S["up2_done"], b.count(1, -1))
                src = gates_dram[b.at()].rearrange("o n -> (o n)").partition_broadcast(P)
                sp.dma_start(gate[b.parity][:], src.rearrange("p (g c) -> p g c", g=2)).then_inc(
                    S[f"gate_loaded{b.parity}"], 16)

            def store(b):
                sp.wait_ge(S["out_done"], b.count())
                sp.dma_start(out_dram[b.at()].rearrange("o p t c -> p o t c"), X[:, b.at()]).then_inc(
                    S["stored"], 16)

            sp.wait_ge(S["gates_done"], 1)
            sp.dma_start(gates_dram, gates16[:]).then_inc(S["gates_stored"], 16)
            sp.wait_ge(S["gates_stored"], 16)
            gates(Batch(0))
            gates(Batch(1))
            with sp.Fori(0, NB // 2 - 1) as trip:
                for u in range(2):
                    gates(Batch(2 + u, trip))
                    store(Batch(u, trip))
            store(Batch(NB - 2))
            store(Batch(NB - 1))
            sp.wait_ge(S["stored"], 16 * NB)

        @block.tensor
        def _(pe):
            def mm(out, lhsT, rhs, start=True, stop=True):
                return pe.matmul(out, lhsT, rhs, start=start, stop=stop)

            def free_bank(name, i):
                was = previous_use(name, i.first)
                if was:
                    who, off = was
                    s, per, extra = last_read[who]
                    pe.wait_ge(S[s], (i + off).count(per, extra))

            def mm3(out, lhs, rhs, start=True, stop=True):
                mm(out, lhs[0], rhs[0], start, False)
                mm(out, lhs[0], rhs[1], False, False)
                return mm(out, lhs[1], rhs[0], False, stop)

            def modulations(parts, which, done):
                for m, part in enumerate(parts):
                    for n in range(NH):
                        for k in range(NH):
                            col = part * E + n * P
                            last = mm(mod_ps(which)[:, m, n], wmod[:, k, col:col + P], csilu[:, k, :],
                                      k == 0, k == NH - 1)
                last.then_inc(S[done], 1)

            def gates():
                for g in range(2):
                    for k in range(NH):
                        last = mm(gate_ps[:, g * E:(g + 1) * E], csilu[:, k, :],
                                  wmod[:, k, (2 + 3 * g) * E:(3 + 3 * g) * E], k == 0, k == NH - 1)
                last.then_inc(S["gate_ps"], 1)

            pe.wait_ge(S["c_silu"], 1)
            pe.wait_ge(S["wmod1_loaded"], 16)
            modulations((0, 1), 0, "mod1_ps")

            def t1(i):
                b = i + 2
                free_bank("t1", i)
                if b.first == 0:
                    pe.wait_ge(S["ident_loaded"], 16)
                pe.wait_ge(S["xn_done"], b.count())
                for n in range(NH):
                    for t in range(NT):
                        c = (n * NT + t) * P
                        last = pe.transpose(bank("t1")[:, c:c + P], xn[b.parity][:, t, n * P:(n + 1) * P], ident[:])
                last.then_inc(S["t1_ps"], 1)

            def qk(i, t):
                b = i + 1
                free_bank(f"qk{t}", i)
                pe.wait_ge(S["hT_split"], b.count())
                if b.first == 0:
                    pe.wait_ge(S["w_lo"], 1)
                for n in range(NH):
                    last = mm3(bank(f"qk{t}"), [x[:, n, t * P:(t + 1) * P] for x in hT_s[b.parity]],
                               [w[:, n, 0:2 * E] for w in wqkv_s], n == 0, n == NH - 1)
                last.then_inc(S["qk_ps"], 1)

            def values(i):
                b = i + 1
                free_bank("v", i)
                for t in range(NT):
                    for n in range(NH):
                        last = mm3(bank("v")[:, t * E:(t + 1) * E],
                                   [x[:, n, t * P:(t + 1) * P] for x in hT_s[b.parity]],
                                   [w[:, n, 2 * E:3 * E] for w in wqkv_s], n == 0, n == NH - 1)
                last.then_inc(S["v_ps"], 1)

            def t2(i, t):
                b = i + 1
                free_bank(f"tk{t}", i)
                pe.wait_ge(S["ks_done"], b.count(2, t + 1))
                for g in range(G):
                    src = ks[t][:, g * HG:(g + 1) * HG].rearrange("p h c d -> p (h c d)").bitcast(F32)
                    last = pe.transpose(bank(f"tk{t}")[:, g * P:(g + 1) * P], src, ident[:])
                last.then_inc(S["tk_ps"], 1)
                free_bank(f"tq{t}", i)
                pe.wait_ge(S["rotadd"], b.count(2, t + 1))
                pe.wait_ge(S["plain_done"], b.count(2, t + 1))
                for g in range(G):
                    src = qr[t][:, g * HG:(g + 1) * HG].rearrange("p h c d -> p (h c d)")
                    last = pe.transpose(bank(f"tq{t}")[:, g * P:(g + 1) * P], src, ident[:])
                last.then_inc(S["tq_ps"], 1)

            def v_heads(b, c, n):
                return v[b.parity][:, c, 4 * n:4 * n + 4].rearrange("p w (x d) -> p w x d", x=3)[:, :, 0:3:2, :]

            def kv(i):
                b = i + 1
                free_bank("kv", i)
                pe.wait_ge(S["kd_done"], b.count())
                pe.wait_ge(S["v_done"], b.count())
                for n in range(NH):
                    lhsT = kd[b.parity][:, 8 * n:8 * n + 8].rearrange("p h d -> p (h d)")
                    mm(bank("kv")[:, n * P:(n + 1) * P], lhsT, v_heads(b, 0, n))
                pe.wait_ge(S["qd_done"], b.count())
                for n in range(NH):
                    src = qd[b.parity][:, 8 * n:8 * n + 8].rearrange("p h d -> p (h d)")
                    last = pe.transpose(bank("kv")[:, E + n * P:E + (n + 1) * P], src, ident[:])
                last.then_inc(S["kv_ps"], 1)

            def scores(b, n):
                c, gp = n // 2, n % 2
                if b.first * 4 + n >= 2:
                    pe.wait_ge(S["pT_done"], b.count(4, n - 1))
                elif n == 0:
                    pe.wait_ge(S["mod1_done"], 1)
                    pe.wait_ge(S["mod2_done"], 1)
                    pe.wait_ge(S["gate_tmp"], 3)
                pe.wait_ge(S["kT_done"], b.count(2, c + 1))
                pe.wait_ge(S["qlo_done"], b.count(2, c + 1))
                for g2 in range(2):
                    for x in range(2):
                        for j in range(2):
                            rows = slice(64 * j, 64 * j + 64)
                            g = 2 * gp + g2
                            last = mm(sc_ps[:, 2 * gp + j, g2], kT[b.parity][rows, c, g, :],
                                      q_s[b.parity][x][rows, c, g], x == 0, x == 1)
                last.then_inc(S["sc_done"], 1)

            def inter(b):
                pe.wait_ge(S["state_done"], b.count())
                pe.wait_ge(S["qdT_done"], b.count())
                if b.first > 0:
                    pe.wait_ge(S["aT_done"], b.count(1, 0))
                for n in range(NH):
                    pe.matmul(o_ps[:, n, P:2 * P], state[b.parity][:, n, :], qdT[b.parity][:, n, :],
                              start=(n == 0), stop=False, skip_group_check=True)

            def pv(b, n):
                c, gp = n // 2, n % 2
                pe.wait_ge(S["pT_done"], b.count(4, n + 1))
                for ab in range(2):
                    for g2 in range(2):
                        for j in range(2):
                            strip = 2 * g2 + j
                            last = pe.matmul(o_ps[32 * strip:32 * strip + 32, gp, c * P:(c + 1) * P],
                                             v[b.parity][:, c, 4 * gp + strip, D * ab:D * ab + 2 * D],
                                             pT[gp][:, j, g2, ab, :], start=False, stop=(ab == 1),
                                             skip_group_check=True)
                last.then_inc(S["pv_done"], 1)

            def t5(i):
                b = i + -2
                free_bank("t5", i)
                pe.wait_ge(S["z_done"], b.count())
                for t in range(NT):
                    last = pe.transpose(bank("t5")[:, t * P:(t + 1) * P], z[b.parity][:, t, :], ident[:])
                last.then_inc(S["t5_ps"], 1)

            def sum_squares(i):
                b = i + -1
                free_bank("ss", i)
                pe.wait_ge(S["sqr_done"], b.count())
                for t in range(NT):
                    last = mm(bank("ss")[:, t:t + 1], sqr[b.parity][:, 0, t * P:(t + 1) * P], ones[:])
                last.then_inc(S["ss_ps"], 1)

            def out_proj(i):
                b = i + -1
                free_bank("wo", i)
                pe.wait_ge(S["aT_done"], b.count())
                if b.first == 0:
                    pe.wait_ge(S["w_lo"], 4)
                for t in range(NT):
                    for n in range(NH):
                        last = mm3(bank("wo")[:, t * E:(t + 1) * E], [x[:, n, t * P:(t + 1) * P] for x in aT_s[b.parity]],
                                   [w[:, n, :] for w in wo_s], n == 0, n == NH - 1)
                last.then_inc(S["wo_ps"], 1)

            def t4(i):
                b = i + -1
                free_bank("t4", i)
                pe.wait_ge(S["xm_done"], b.count())
                for n in range(NH):
                    for t in range(NT):
                        c = (n * NT + t) * P
                        last = pe.transpose(bank("t4")[:, c:c + P], xm[b.parity][:, t, n * P:(n + 1) * P], ident[:])
                last.then_inc(S["t4_ps"], 1)

            def f1(i):
                b = i + -1
                free_bank("f1", i)
                pe.wait_ge(S["h2T_done"], b.count())
                if b.first == 0:
                    pe.wait_ge(S["w2_loaded"], 16 * 4)
                for t in range(NT):
                    for n in range(NH):
                        last = mm(bank("f1")[:, t * (NA + NE):(t + 1) * (NA + NE)], h2T[:, n, t * P:(t + 1) * P],
                                  war[:, n, :], n == 0, n == NH - 1)
                last.then_inc(S["f1_ps"], 1)

            def base(i):
                b = i + -2
                if b.first < NB - 1:
                    free_bank("f2", i)
                pe.wait_ge(S["h2T_split"], b.count())
                for t in range(NT):
                    for n in range(NH):
                        lhs, rhs = [x[:, n, t * P:(t + 1) * P] for x in h2T_s[b.parity]], [w[:, n, :] for w in wbase_s]
                        for x, y in ((0, 0), (0, 1), (1, 0)):
                            pe.matmul(f2_ps(b)[:, t * E:(t + 1) * E], lhs[x], rhs[y],
                                      start=(t + n + x + y == 0), stop=False, skip_group_check=True)

            def lora_b(i):
                b = i + -2
                pe.wait_ge(S["zlo_done"], b.count())
                for t in range(NT):
                    for x, y in ((0, 0), (0, 1), (1, 0)):
                        last = pe.matmul(f2_ps(b)[:, t * E:(t + 1) * E], zT_s[b.parity][x][:, t * P:(t + 1) * P],
                                         wb_s[y][:], start=False, stop=(x == 1), skip_group_check=True)
                last.then_inc(S["f2_ps"], 1)

            def iteration(i):
                front, mid, back, tail = i + 1, i, i + -1, i + -2
                if back.on:
                    pv(back, 3)
                if mid.on:
                    scores(mid, 0)
                if (i + 2).on:
                    t1(i)
                if mid.on:
                    scores(mid, 1)
                if back.on:
                    sum_squares(i)
                    out_proj(i)
                last_tail = tail.first == NB - 1
                if last_tail:
                    base(i)
                if tail.on:
                    t5(i)
                if front.on:
                    qk(i, 0)
                if mid.on:
                    inter(mid)
                    pv(mid, 0)
                if front.on:
                    qk(i, 1)
                if tail.on:
                    if not last_tail:
                        base(i)
                    lora_b(i)
                if front.on:
                    values(i)
                if back.on and front.on:
                    t4(i)
                if mid.on:
                    scores(mid, 2)
                if back.on and not front.on:
                    t4(i)
                if front.on:
                    t2(i, 0)
                if front.first == 0:
                    pe.wait_ge(S["wmod2_loaded"], 16)
                    modulations((3, 4), 1, "mod2_ps")
                    gates()
                if mid.on:
                    pv(mid, 1)
                    scores(mid, 3)
                if back.on:
                    f1(i)
                if mid.on:
                    pv(mid, 2)
                if front.on:
                    t2(i, 1)
                    kv(i)

            pipeline(pe, iteration, -2, NB + 1)

        @block.scalar
        def _(act):
            act.dma_start(ident[:], a["ident"]).then_inc(S["ident_loaded"], 16)
            act.wait_ge(S["c_loaded"], 16)
            act.activation(ctmp[:, 0], cT[:], ACT.Exp, scale=-1.0).then_inc(S["c_exp"], 1)
            loads = (("rcos", rcos), ("rsin", rsin), ("qdecay", qdecay), ("kdecay", kdecay),
                     ("even_odd", even_odd), ("rms_w", rmsw), ("diag", diag), ("least", least))
            for name, dst in loads:
                act.dma_start(dst[:], a[name]).then_inc(S["consts_loaded"], 16)
            act.wait_ge(S["mod1_done"], 1)

            def h_evac(b, src, full, hi, shift, scale, ready, split, done):
                act.wait_ge(S[ready], b.count())
                if b.first > 0:
                    act.wait_ge(S[split], b.count(1, 0))
                k = b.at()
                for dst in (full, hi):
                    for n in range(NH):
                        last = act.activation(dst[:, n, :], src[:, n * NT * P:(n + 1) * NT * P], ACT.Identity,
                                              bias=modT[:, shift, n, k], scale=modT[:, scale, n, k])
                last.then_inc(S[done], 1)

            def plain_dims(i, t):
                b = i + 1
                qkv = bank(f"qk{t}").rearrange("p (w h d) -> p w h d", w=2, d=D)
                act.wait_ge(S["rotmul"], b.count(2, t + 1))
                act.activation(kr[t][:, :, 8:16], qkv[:, 1, :, 8:16], ACT.Copy)
                act.activation(qr[t][:, :, :, 8:16], qkv[:, 0, :, 8:16].unsqueeze(2).broadcast_to([P, H, 2, 8]),
                               ACT.Copy).then_inc(S["plain_done"], 1)

            def k_high(i, t):
                b = i + 1
                act.wait_ge(S["rotadd"], b.count(2, t + 1))
                act.wait_ge(S["plain_done"], b.count(2, t + 1))
                act.activation(ks[t][:, :, 0, :], kr[t][:], ACT.Copy).then_inc(S["khi_done"], 1)

            def values_evac(b):
                act.wait_ge(S["v_ps"], b.count())
                for t in range(NT):
                    dst = v[b.parity][:, t].rearrange("p w (x d) -> p w x d", x=3)[:, :, 0:3:2, :]
                    last = act.activation(dst, bank("v")[:, t * E:(t + 1) * E].rearrange(
                        "p (w x d) -> p w x d", x=2, d=D), ACT.Copy)
                last.then_inc(S["v_done"], 1)

            def q_high(b, t):
                act.wait_ge(S["tq_ps"], b.count(2, t + 1))
                for ab in range(2):
                    last = act.activation(q_s[b.parity][0][:, t, :, ab, :],
                                          bank(f"tq{t}").rearrange("p (g c) -> p g c", g=G), ACT.Copy,
                                          scale=even_odd[:, ab:ab + 1])
                last.then_inc(S["qhi_done"], 1)

            def k_evac(b, t):
                act.wait_ge(S["tk_ps"], b.count(2, t + 1))
                act.activation(kT[b.parity][:, t], bank(f"tk{t}").rearrange("p (g c) -> p g c", g=G),
                               ACT.Copy).then_inc(S["kT_done"], 1)

            def iteration(i):
                front, mid, back, tail, ahead_b = i + 1, i, i + -1, i + -2, i + 2
                if mid.on:
                    act.wait_ge(S["kv_ps"], mid.count())
                    act.activation(qdT[mid.parity][:], bank("kv")[:, E:2 * E].rearrange("p (n c) -> p n c", n=NH),
                                   ACT.Copy).then_inc(S["qdT_done"], 1)
                if back.on:
                    act.wait_ge(S["pv_done"], back.count(4, 4))
                    act.activation(sqr[back.parity][:], o_ps[:], ACT.Square).then_inc(S["o_copied"], 1)
                    act.activation(aT_s[back.parity][0][:], o_ps[:], ACT.Copy).then_inc(S["o_copied"], 1)
                if tail.on:
                    act.wait_ge(S["lsub_done"], tail.count())
                    act.activation(lexp[:, tail.parity], lsub[:, tail.parity], ACT.Exp).then_inc(S["lexp_done"], 1)
                if ahead_b.on:
                    h_evac(ahead_b, bank("t1"), hT, hT_s[ahead_b.parity][0], SA, CA, "t1_ps", "hT_split", "hT_done")
                if tail.on:
                    act.wait_ge(S["t5_ps"], tail.count())
                    act.activation(zT_s[tail.parity][0][:], bank("t5")[:, 0:NT * P], ACT.Copy).then_inc(S["zhi_done"], 1)
                if front.on:
                    plain_dims(i, 0)
                    k_high(i, 0)
                    plain_dims(i, 1)
                    values_evac(front)
                if back.on:
                    h_evac(back, bank("t4"), h2T, h2T_s[back.parity][0], SB, CB, "t4_ps", "h2T_split", "h2T_done")
                if front.on:
                    k_high(i, 1)
                    q_high(front, 0)
                    k_evac(front, 0)
                if back.on:
                    act.wait_ge(S["f1_ps"], back.count())
                    if back.first >= 2:
                        act.wait_ge(S["z_done"], back.count(1, -1))
                    act.activation(f1s[:, back.parity], bank("f1")[:, 0:NT * (NA + NE)].rearrange(
                        "p (t c) -> p t c", t=NT), ACT.Copy).then_inc(S["lg_done"], 1)
                if front.on:
                    k_evac(front, 1)
                    q_high(front, 1)

            pipeline(act, iteration, -2, NB + 1)

        @block.gpsimd
        def _(pool):
            pool.memset(minus_half[:], -0.5).then_inc(S["const_done"], 1)
            pool.memset(ones[:], 1.0)
            for p in range(2):
                pool.memset(v[p][:], 0.0)
            pool.wait_ge(S["const_done"], 1)

            def scale_wo():
                pool.wait_ge(S["w2_loaded"], 16 * 4)
                pool.wait_ge(S["consts_loaded"], 16 * 8)
                for n in range(NH):
                    last = pool.tensor_scalar(wo[:, n, :], wo_in[:, n, :], rmsw[:, n:n + 1], None, ALU.mult)
                last.then_inc(S["wo_scaled"], 1)

            def rsqrt(b, var, tmp, out, ready, added, done):
                hold(pool, S[ready], b.count(), S["pool_held"])
                pool.tensor_scalar(tmp, var, 1.0, EPS, ALU.mult, ALU.add).then_inc(S[added], 1)
                pool.wait_ge(S[added], b.count())
                pool.tensor_tensor(out, tmp, minus_half[:], ALU.pow).then_inc(S[done], 1)

            def rotate(i, t):
                b = i + 1
                pool.wait_ge(S["rotmul"], b.count(2, t + 1))
                pool.tensor_tensor(kr[t][:, :, 0:8], rotc[t][:, H:2 * H, :], rots[t][:, H:2 * H, :], ALU.add)
                pool.tensor_tensor(qr[t][:, :, :, 0:8], rotc[t][:, 0:H, :].unsqueeze(2).broadcast_to([P, H, 2, 8]),
                                   rots[t][:, 0:H, :].unsqueeze(2).broadcast_to([P, H, 2, 8]),
                                   ALU.add).then_inc(S["rotadd"], 1)

            def k_low(i, t):
                b = i + 1
                pool.wait_ge(S["rotadd"], b.count(2, t + 1))
                pool.wait_ge(S["khi_done"], b.count(2, t + 1))
                pool.tensor_tensor(ks[t][:, :, 1, :], kr[t][:], ks[t][:, :, 0, :].bitcast(F32),
                                   ALU.subtract).then_inc(S["ks_done"], 1)
                if t == 0:
                    pool.tensor_tensor(kd[b.parity][:], kr[0][:], kdecay[:].unsqueeze(2).broadcast_to([P, H, D]),
                                       ALU.mult).then_inc(S["kd_done"], 1)
                else:
                    pool.tensor_tensor(qd[b.parity][:], qr[1][:, :, 0, :], qdecay[:].unsqueeze(2).broadcast_to([P, H, D]),
                                       ALU.mult).then_inc(S["qd_done"], 1)

            def h_low(b, full, split, ready, done):
                pool.wait_ge(S[ready], b.count())
                pool.tensor_tensor(split[1][:], full[:], split[0][:].bitcast(F32), ALU.subtract).then_inc(S[done], 1)

            def iteration(i):
                front, back, tail, ahead_b, stats_b = i + 1, i + -1, i + -2, i + 2, i + 3
                p = back.parity
                if back.on:
                    pool.wait_ge(S["o_copied"], back.count(2, 1))
                    pool.tensor_tensor(sqr[p][:, 0], sqr[p][:, 0], sqr[p][:, 1], ALU.add).then_inc(S["sqr_done"], 1)
                    pool.wait_ge(S["ms_done"], back.count())
                    pool.tensor_tensor(rrms[:, p], ms[:, p], minus_half[:], ALU.pow).then_inc(S["rrms_done"], 1)
                    hold(pool, S["up_done"], back.count(), S["pool_held"])
                    pool.tensor_tensor(X[:, back.at()], X[:, back.at()], up[back.parity].unsqueeze(1),
                                       ALU.add).then_inc(S["x1_done"], 1)
                if front.on:
                    rotate(i, 0)
                if back.on:
                    rsqrt(back, mv2[:, p, :, 1], ve2[:, p], rstd2[:, p], "mean2", "ve2_done", "rstd2_done")
                if front.on:
                    k_low(i, 0)
                    rotate(i, 1)
                if stats_b.on:
                    q = stats_b.parity
                    rsqrt(stats_b, mv1[:, q, :, 1], ve1[:, q], rstd1[:, q], "mean1", "ve1_done", "rstd1_done")
                if tail.on:
                    hold(pool, S["up2_done"], tail.count(), S["pool_held"])
                    pool.tensor_tensor(X[:, tail.at()], X[:, tail.at()], up2[tail.parity][:].unsqueeze(1),
                                       ALU.add).then_inc(S["out_done"], 1)
                if front.on:
                    k_low(i, 1)
                if back.on:
                    h_low(back, h2T, h2T_s[p], "h2T_done", "h2T_split")
                    pool.wait_ge(S["lg_done"], back.count())
                    if back.first > 0:
                        pool.wait_ge(S["ahead_done"], back.count(1, 0))
                    pool.tensor_tensor(ldiff[:], lg[:, p].unsqueeze(2).broadcast_to([P, NT, NE, NE]),
                                       lg[:, p].unsqueeze(3).broadcast_to([P, NT, NE, NE]),
                                       ALU.subtract).then_inc(S["ldiff_done"], 1)
                if ahead_b.on:
                    h_low(ahead_b, hT, hT_s[ahead_b.parity], "hT_done", "hT_split")
                if ahead_b.first == 1:
                    scale_wo()

            pipeline(pool, iteration, -3, NB + 1)

        @block.vector
        def _(dve):
            dve.wait_ge(S["c_exp"], 1)
            dve.tensor_scalar(ctmp[:, 1], ctmp[:, 0], 1.0, None, ALU.add).then_inc(S["c_tmp"], 1)
            dve.wait_ge(S["c_tmp"], 1)
            dve.reciprocal(ctmp[:, 2], ctmp[:, 1]).then_inc(S["c_tmp"], 1)
            dve.wait_ge(S["c_tmp"], 2)
            dve.tensor_tensor(csilu[:], cT[:], ctmp[:, 2], ALU.mult).then_inc(S["c_silu"], 1)

            def take_modulations(which):
                dve.wait_ge(S[f"mod{which + 1}_ps"], 1)
                dve.tensor_scalar(modT[:, 2 * which], mod_ps(which)[:, 0], 0.0, None, ALU.add)
                dve.tensor_scalar(modT[:, 2 * which + 1], mod_ps(which)[:, 1], 1.0, None, ALU.add).then_inc(
                    S[f"mod{which + 1}_done"], 1)

            def take_gates():
                dve.wait_ge(S["gate_ps"], 1)
                dve.tensor_scalar(gstep[:], gate_ps, 0.0, 2.0, ALU.is_ge, ALU.mult).then_inc(S["gate_tmp"], 1)
                dve.wait_ge(S["gate_tmp"], 1)
                dve.tensor_scalar(gsign[:], gstep[:], -1.0, None, ALU.add).then_inc(S["gate_tmp"], 1)
                dve.wait_ge(S["gate_tmp"], 2)
                dve.tensor_tensor(gmag[:], gate_ps, gsign[:], ALU.mult).then_inc(S["gate_tmp"], 1)
                dve.wait_ge(S["gate_tmp"], 3)
                dve.scalar_tensor_tensor(out=gates16[:], in0=gmag[:], scalar=0.25, in1=gsign[:], op0=ALU.max,
                                         op1=ALU.mult).then_inc(S["gates_done"], 1)

            def stats(x, st, b, stats_sem):
                for t in range(NT):
                    last = dve.bn_stats(st[:, b.parity, t, :], x[:, t, :])
                last.then_inc(S[stats_sem], 1)

            def mean(st, mv, b, stats_sem, mean_sem):
                hold(dve, S[stats_sem], b.count(), S["dve_held"])
                for t in range(NT):
                    last = dve.bn_aggr(mv[:, b.parity, t, :], st[:, b.parity, t, :])
                last.then_inc(S[mean_sem], 1)

            def normalise(x, dst, mv, rstd, b):
                for t in range(NT):
                    last = dve.tensor_scalar(dst[:, t, :], x[:, t, :], mv[:, b.parity, t, 0:1],
                                             rstd[:, b.parity, t:t + 1], ALU.subtract, ALU.mult)
                return last

            def x_of(b):
                return X[:, b.at()].rearrange("p o t c -> p (o t) c")

            def mask(b, n):
                c, r = n // 2, n % 2
                if b.first == 0 and n == 0:
                    dve.wait_ge(S["dmask_loaded"], 16)
                dve.wait_ge(S["sc_done"], b.count(4, n + 1))
                if b.first * 4 + n >= 2:
                    dve.wait_ge(S["pv_done"], b.count(4, n - 1))
                flat = "p j g x t -> p (j g x t)"
                dve.tensor_tensor(pT[r][:].rearrange(flat), sc_ps[:, 2 * r:2 * r + 2].rearrange(flat),
                                  dmask[:, r].rearrange(flat), ALU.mult).then_inc(S["pT_done"], 1)

            def rot(i, t):
                b = i + 1
                dve.wait_ge(S["qk_ps"], b.count(2, t + 1))
                if b.first > 0:
                    dve.wait_ge(S["rotadd"], b.count(2, t - 1))
                qkv = bank(f"qk{t}").rearrange("p (h d) -> p h d", d=D)
                dve.tensor_tensor(rotc[t][:], qkv[:, :, 0:8], rcos[:, t].unsqueeze(1).broadcast_to([P, 2 * H, 8]),
                                  ALU.mult)
                dve.tensor_tensor(rots[t][:, :, 0:4], qkv[:, :, 4:8],
                                  rsin[:, t, 0:4].unsqueeze(1).broadcast_to([P, 2 * H, 4]), ALU.mult)
                dve.tensor_tensor(rots[t][:, :, 4:8], qkv[:, :, 0:4],
                                  rsin[:, t, 4:8].unsqueeze(1).broadcast_to([P, 2 * H, 4]),
                                  ALU.mult).then_inc(S["rotmul"], 1)

            def q_low(i, t):
                b = i + 1
                p = b.parity
                dve.wait_ge(S["qhi_done"], b.count(2, t + 1))
                for ab in range(2):
                    last = dve.scalar_tensor_tensor(
                        out=q_s[p][1][:, t, :, ab, :], in0=bank(f"tq{t}").rearrange("p (g c) -> p g c", g=G),
                        scalar=even_odd[:, ab:ab + 1], in1=q_s[p][0][:, t, :, ab, :].bitcast(F32), op0=ALU.mult,
                        op1=ALU.subtract)
                last.then_inc(S["qlo_done"], 1)

            def ln1_stats(i):
                b = i + 3
                dve.wait_ge(S[f"x_loaded{b.parity}"], b.count(8, 16 - 8 * b.parity))
                stats(x_of(b), stat1, b, "stats1")

            def ln1_apply(i):
                b = i + 3
                dve.wait_ge(S["rstd1_done"], b.count())
                if b.first >= 2:
                    dve.wait_ge(S["t1_ps"], b.count(1, -1))
                normalise(x_of(b), xn[b.parity], mv1, rstd1, b).then_inc(S["xn_done"], 1)

            def split_weights(n, src, dst):
                dve.tensor_copy(dst[0], src).then_inc(S["w_hi"], 1)
                dve.wait_ge(S["w_hi"], n)
                dve.tensor_tensor(dst[1], src, dst[0].bitcast(F32), ALU.subtract).then_inc(S["w_lo"], 1)

            def z_low(b):
                dve.wait_ge(S["zhi_done"], b.count())
                dve.tensor_tensor(zT_s[b.parity][1][:], bank("t5")[:, 0:NT * P], zT_s[b.parity][0][:].bitcast(F32),
                                  ALU.subtract).then_inc(S["zlo_done"], 1)

            def a_low(b):
                dve.wait_ge(S["o_copied"], b.count(2, 2))
                dve.tensor_tensor(aT_s[b.parity][1][:], o_ps[:], aT_s[b.parity][0][:].bitcast(F32),
                                  ALU.subtract).then_inc(S["aT_done"], 1)

            def mean_square(b):
                dve.wait_ge(S["ss_ps"], b.count())
                dve.tensor_scalar(ms[:, b.parity], bank("ss")[:, 0:NT], 1.0 / E, EPS, ALU.mult, ALU.add).then_inc(
                    S["ms_done"], 1)

            def gate_attention(b):
                p = b.parity
                dve.wait_ge(S[f"gate_loaded{p}"], b.count(8, 16 - 8 * p))
                dve.wait_ge(S["wo_ps"], b.count())
                dve.wait_ge(S["rrms_done"], b.count())
                for t in range(NT):
                    last = dve.scalar_tensor_tensor(
                        out=up[p][:, t, :], in0=bank("wo")[:, t * E:(t + 1) * E], scalar=rrms[:, p, t:t + 1],
                        in1=gate[p][:, 0, :], op0=ALU.mult, op1=ALU.mult)
                last.then_inc(S["up_done"], 1)

            def gate_experts(b):
                dve.wait_ge(S["f2_ps"], b.count())
                gb = gate[b.parity][:, 1, :].unsqueeze(1).broadcast_to([P, NT, E])
                dve.tensor_tensor(up2[b.parity][:], f2_ps(b).rearrange("p (t c) -> p t c", t=NT), gb,
                                  ALU.mult).then_inc(S["up2_done"], 1)

            def take_state(b):
                dve.wait_ge(S["kv_ps"], b.count())
                dve.wait_ge(S["qdT_done"], b.count())
                dve.tensor_tensor(state[b.parity][:], bank("kv")[:, 0:E].rearrange("p (n c) -> p n c", n=NH),
                                  diag[:].unsqueeze(1).broadcast_to([P, NH, P]),
                                  ALU.mult).then_inc(S["state_done"], 1)

            def logits_less_max(b):
                p = b.parity
                dve.wait_ge(S["lg_done"], b.count())
                dve.reduce_max(lmax[:, p], lg[:, p], AX_X).then_inc(S["lmax_done"], 1)
                dve.wait_ge(S["lmax_done"], b.count())
                dve.tensor_tensor(lsub[:, p], lg[:, p], lmax[:, p].unsqueeze(2).broadcast_to([P, NT, NE]),
                                  ALU.subtract).then_inc(S["lsub_done"], 1)

            def expert_ranks(b):
                p = b.parity
                dve.wait_ge(S["ldiff_done"], b.count())
                dve.tensor_tensor(ahead[:], ldiff[:], least[:].unsqueeze(1).broadcast_to([P, NT, NE, NE]),
                                  ALU.is_ge).then_inc(S["ahead_done"], 1)
                dve.wait_ge(S["ahead_done"], b.count())
                dve.reduce_sum(rank[:, p], ahead[:], AX_X).then_inc(S["rank_done"], 1)

            def route(b):
                p = b.parity
                dve.wait_ge(S["rank_done"], b.count())
                dve.wait_ge(S["lexp_done"], b.count())
                dve.scalar_tensor_tensor(out=wsel[:, p], in0=rank[:, p], scalar=2.0, in1=lexp[:, p],
                                         op0=ALU.is_lt, op1=ALU.mult).then_inc(S["wsel_done"], 1)
                dve.wait_ge(S["wsel_done"], b.count())
                dve.reduce_sum(wsum[:, p], wsel[:, p], AX_X).then_inc(S["wsum_done"], 1)
                dve.wait_ge(S["wsum_done"], b.count())
                dve.reciprocal(wrec[:, p], wsum[:, p]).then_inc(S["wrec_done"], 1)
                dve.wait_ge(S["wrec_done"], b.count())
                dve.scalar_tensor_tensor(out=wexp[:, p], in0=wsel[:, p], scalar=SCALING,
                                         in1=wrec[:, p].unsqueeze(2).broadcast_to([P, NT, NE]),
                                         op0=ALU.mult, op1=ALU.mult).then_inc(S["wexp_done"], 1)
                dve.wait_ge(S["wexp_done"], b.count())
                dve.tensor_tensor(z[p][:].rearrange("p t (e r) -> p t e r", r=R),
                                  f1s[:, p, :, 0:NA].rearrange("p t (e r) -> p t e r", r=R),
                                  wexp[:, p].unsqueeze(3).broadcast_to([P, NT, NE, R]),
                                  ALU.mult).then_inc(S["z_done"], 1)

            def iteration(i):
                front, mid, back, tail = i + 1, i, i + -1, i + -2
                pb = back.parity
                if mid.on:
                    take_state(mid)
                if back.on:
                    a_low(back)
                if tail.on:
                    route(tail)
                if back.on:
                    mean_square(back)
                if mid.on:
                    mask(mid, 0)
                if back.on:
                    gate_attention(back)
                if tail.on:
                    z_low(tail)
                if mid.on:
                    mask(mid, 1)
                if front.on:
                    rot(i, 0)
                if back.on:
                    dve.wait_ge(S["x1_done"], back.count())
                    stats(x_of(back), stat2, back, "stats2")
                    mean(stat2, mv2, back, "stats2", "mean2")
                if front.on:
                    rot(i, 1)
                if front.first == 0:
                    dve.wait_ge(S["w2_loaded"], 16 * 4)
                    split_weights(2, wbase[:], [w[:] for w in wbase_s])
                    split_weights(3, wb[:], [w[:] for w in wb_s])
                if back.on:
                    dve.wait_ge(S["rstd2_done"], back.count())
                    normalise(x_of(back), xm[pb], mv2, rstd2, back).then_inc(S["xm_done"], 1)
                if tail.on:
                    gate_experts(tail)
                if (i + 3).on:
                    ln1_stats(i)
                    mean(stat1, mv1, i + 3, "stats1", "mean1")
                if mid.on:
                    mask(mid, 2)
                if i.first == -2:
                    take_modulations(0)
                if (i + 3).on:
                    ln1_apply(i)
                if front.on:
                    q_low(i, 0)
                if mid.on:
                    mask(mid, 3)
                if back.on:
                    logits_less_max(back)
                    expert_ranks(back)
                if front.first == 0:
                    take_modulations(1)
                    take_gates()
                if mid.first == 0:
                    dve.wait_ge(S["wo_scaled"], 1)
                    split_weights(4, wo[:], [w[:] for w in wo_s])
                if front.on:
                    q_low(i, 1)
                if i.first == -2:
                    dve.wait_ge(S["wqkv_loaded"], 16)
                    split_weights(1, wqkv[:], [w[:] for w in wqkv_s])
                    dve.wait_ge(S["consts_loaded"], 16 * 8)

            pipeline(dve, iteration, -3, NB + 1)


def shape_tables():
    import math

    import numpy as np

    f = np.float32
    start = 2.0 ** (-2.0 ** (-(math.log2(H) - 3)))
    slopes = np.array([start * start ** i for i in range(H)], dtype=f)
    r = np.exp(-slopes.astype(np.float64)).astype(f).astype(np.float64)
    i = np.arange(P, dtype=np.float64)
    diff = i[None, :] - i[:, None]
    decay = np.where(diff[None] >= 0, r[:, None, None] ** np.maximum(diff, 0)[None], 0.0)
    dmask = decay.reshape(2, 2, 2, 2, P, P).transpose(4, 0, 2, 1, 3, 5)
    freq = np.concatenate([(f(1.0 / 1024.0) ** np.linspace(0.0, 1.0, D // 4, dtype=f)).astype(f)])
    theta = (np.arange(NT * P, dtype=f)[:, None] * freq[None, :]).astype(f).astype(np.float64)
    cos, sin = np.cos(theta), np.sin(theta)
    rcos = np.concatenate([cos, cos], axis=1).reshape(NT, P, 8).transpose(1, 0, 2)
    rsin = np.concatenate([sin, -sin], axis=1).reshape(NT, P, 8).transpose(1, 0, 2)
    row = np.arange(P)
    diag = row[:, None] // D == row[None, :] // D
    even_odd = np.stack([row // 32 % 2 == 0, row // 32 % 2 == 1], axis=1)
    e = np.arange(NE)
    ej = e[None, :] - e[:, None]
    least = np.broadcast_to(np.where(ej < 0, 0.0, np.where(ej > 0, np.finfo(f).tiny, np.finfo(f).max)), (P, NE, NE))
    return {k: np.ascontiguousarray(t, dtype=f) for k, t in {
        "dmask": dmask, "qdecay": (r[:, None] ** (i[None] + 1.0)).T, "kdecay": (r[:, None] ** (P - 1.0 - i[None])).T,
        "rcos": rcos, "rsin": rsin, "ident": np.eye(P), "diag": diag, "even_odd": even_odd, "least": least}.items()}


def kernel(**inputs):
    import numpy as np
    import concourse.bacc as bacc
    from concourse.bass_utils import run_bass_kernel_spmd as run

    f = {k[3:]: np.asarray(t) for k, t in inputs.items()}
    order = np.concatenate([np.r_[0:4, 8:12, 4:8, 12:16] + D * h for h in range(H)])
    arrays = {
        "x": f["attn_x"], "cT": f["c"].T, "wmod": f["wmod"],
        "wqkv": np.concatenate([f["attn_Wq"][:, order], f["attn_Wk"][:, order], f["attn_Wv"]], axis=1),
        "wo": f["attn_Wo"], "rms_w": f["attn_rms_w"].reshape(NH, P).T,
        "war": np.concatenate([f["ffn_lora_A"].reshape(NA, E).T, f["ffn_router_w"].T], axis=1),
        "wbase": f["ffn_weight"].T, "wb": f["ffn_lora_B"].transpose(0, 2, 1).reshape(NA, E),
    }
    arrays.update(shape_tables())
    arrays = {f"in_{k}": np.ascontiguousarray(t) for k, t in arrays.items()}
    nc = bacc.Bacc("TRN2", target_bir_lowering=False, num_devices=1)
    a = {k[3:]: nc.dram_tensor(k, t.shape, mybir.dt.from_np(t.dtype), kind="ExternalInput").ap()
         for k, t in arrays.items()}
    a["out"] = nc.dram_tensor("out_0", (NB, NT * P, E), F32, kind="ExternalOutput").ap()
    build(nc, a)
    r = run(nc, [arrays], core_ids=[0])
    return r.results[0]["out_0"]
```
